# Optimizing a Trainium2 kernel written in Bass

```python
import numpy as np
import jax
import jax.numpy as jnp

def _softmax(x, axis=-1):
    return jax.nn.softmax(x, axis=axis)

def _gelu(x):
    return jax.nn.gelu(x, approximate=True)

def _silu(x):
    return jax.nn.silu(x)

def _sigmoid(x):
    return jax.nn.sigmoid(x)

def _layernorm(x, axis=-1, eps=1e-05):
    m = jnp.mean(x, axis=axis, keepdims=True)
    v = jnp.var(x, axis=axis, keepdims=True)
    return (x - m) / jnp.sqrt(v + eps)

def _scatter_add(tgt, idx, src, axis=0):
    return tgt.at[idx].add(src)

def _segment_sum(src, seg, n):
    return jax.ops.segment_sum(src, seg, n)
kernel_name = 'mk_adj_ffn_d1_adj_r2_f91e2a'

def setup_inputs(seed: int=0):
    np.random.seed(seed)
    _w = jnp.asarray

    def _rec_inputs():
        import jax
        import jax.numpy as jnp
        _gk = jax.random.key(seed)
        x = -0.0001538 + 1 * jax.random.normal(jax.random.fold_in(_gk, 1), (64, 128, 384), jnp.float32)
        _a = jax.random.bernoulli(jax.random.fold_in(_gk, 2), 0.0625, (64, 128, 128))
        _a = jnp.logical_or(_a, jnp.swapaxes(_a, -1, -2))
        _a = jnp.logical_or(_a, jnp.eye(128, dtype=bool))
        _af = _a.astype(jnp.float32)
        _af = _af * jax.random.uniform(jax.random.fold_in(_gk, 3), (64, 128, 128), jnp.float32, 0.05, 4.42607)
        adj = _af
        return (x, adj)
    x, adj = _rec_inputs()

    def _L0_gnn_setup():
        import jax, jax.numpy as jnp
        import numpy as np
        NUM_HEADS = 12
        HIDDEN = 384
        HEAD = HIDDEN // NUM_HEADS
        SCALE = HIDDEN ** (-0.5)
        key = jax.random.key(seed)
        ks = jax.random.split(key, 8)
        B, N = (16, 256)
        std = HIDDEN ** (-0.5)
        return {'x': jax.random.normal(ks[0], (B, N, HIDDEN), dtype=jnp.float32), 'encoding_bias': jax.random.normal(ks[1], (B, N, N), dtype=jnp.float32), 'Wq': jax.random.normal(ks[2], (HIDDEN, HIDDEN), dtype=jnp.float32) * std, 'Wk': jax.random.normal(ks[3], (HIDDEN, HIDDEN), dtype=jnp.float32) * std, 'Wv': jax.random.normal(ks[4], (HIDDEN, HIDDEN), dtype=jnp.float32) * std, 'bv': jax.random.normal(ks[5], (HIDDEN,), dtype=jnp.float32) * 0.01, 'Wo': jax.random.normal(ks[6], (HIDDEN, HIDDEN), dtype=jnp.float32) * std, 'bo': jax.random.normal(ks[7], (HIDDEN,), dtype=jnp.float32) * 0.01}
    _L0_gnn_all = _L0_gnn_setup()
    _L0_gnn_in = {k: v for k, v in _L0_gnn_all.items() if k in ('Wq', 'Wk', 'Wv', 'bv', 'Wo', 'bo')}
    del _L0_gnn_all

    def _L0_ffn_setup():
        import jax, jax.numpy as jnp
        import numpy as np
        B, L, D, E, TOP_K = (8, 512, 384, 4, 2)
        H = 2 * D
        LN_EPS = 1e-05

        def _gelu(v):
            return jax.nn.gelu(v, approximate=False)

        def _mish(v):
            return v * jnp.tanh(jax.nn.softplus(v))
        _ACTS = [_gelu, jax.nn.silu, _mish, _gelu]
        key = jax.random.key(seed)
        ks = jax.random.split(key, 8)
        x = jax.random.normal(ks[0], (B, L, D), dtype=jnp.float32)
        router_w = jax.random.normal(ks[1], (E, D), dtype=jnp.float32) * 0.02
        router_b = jnp.zeros((E,), dtype=jnp.float32)
        w1 = jax.random.normal(ks[2], (E, D, H), dtype=jnp.float32) * (1.0 / np.sqrt(D))
        b1 = jax.random.normal(ks[3], (E, H), dtype=jnp.float32) * 0.01
        w2 = jax.random.normal(ks[4], (E, H, D), dtype=jnp.float32) * (1.0 / np.sqrt(H))
        b2 = jax.random.normal(ks[5], (E, D), dtype=jnp.float32) * 0.01
        ln_g = jnp.ones((D,), dtype=jnp.float32)
        ln_b = jnp.zeros((D,), dtype=jnp.float32)
        return {'x': x, 'router_w': router_w, 'router_b': router_b, 'w1': w1, 'b1': b1, 'w2': w2, 'b2': b2, 'ln_g': ln_g, 'ln_b': ln_b}
    _L0_ffn_all = _L0_ffn_setup()
    _L0_ffn_in = {k: v for k, v in _L0_ffn_all.items() if k in ('router_w', 'router_b', 'w1', 'b1', 'w2', 'b2', 'ln_g', 'ln_b')}
    del _L0_ffn_all
    return {'x': x, 'adj': adj, 'L0_gnn_Wq': _L0_gnn_in['Wq'], 'L0_gnn_Wk': _L0_gnn_in['Wk'], 'L0_gnn_Wv': _L0_gnn_in['Wv'], 'L0_gnn_bv': _L0_gnn_in['bv'], 'L0_gnn_Wo': _L0_gnn_in['Wo'], 'L0_gnn_bo': _L0_gnn_in['bo'], 'L0_ffn_router_w': _L0_ffn_in['router_w'], 'L0_ffn_router_b': _L0_ffn_in['router_b'], 'L0_ffn_w1': _L0_ffn_in['w1'], 'L0_ffn_b1': _L0_ffn_in['b1'], 'L0_ffn_w2': _L0_ffn_in['w2'], 'L0_ffn_b2': _L0_ffn_in['b2'], 'L0_ffn_ln_g': _L0_ffn_in['ln_g'], 'L0_ffn_ln_b': _L0_ffn_in['ln_b']}

def reference(x, adj, L0_gnn_Wq, L0_gnn_Wk, L0_gnn_Wv, L0_gnn_bv, L0_gnn_Wo, L0_gnn_bo, L0_ffn_router_w, L0_ffn_router_b, L0_ffn_w1, L0_ffn_b1, L0_ffn_w2, L0_ffn_b2, L0_ffn_ln_g, L0_ffn_ln_b):
    import jax
    import jax.numpy as jnp

    def _L0_gnn_ref(x, encoding_bias, Wq, Wk, Wv, bv, Wo, bo):
        import jax, jax.numpy as jnp
        import numpy as np
        NUM_HEADS = 12
        HIDDEN = 384
        HEAD = HIDDEN // NUM_HEADS
        SCALE = HIDDEN ** (-0.5)
        B, N, _ = x.shape
        q = (x @ Wq.T).reshape(B, N, NUM_HEADS, HEAD)
        k = (x @ Wk.T).reshape(B, N, NUM_HEADS, HEAD)
        v = (x @ Wv.T + bv).reshape(B, N, NUM_HEADS, HEAD)
        a = jnp.einsum('bnhd,bmhd->bhnm', q, k) * SCALE + encoding_bias[:, None, :, :]
        pad_mask = jnp.all(a == 0, axis=-1)
        a = jnp.where(pad_mask[..., None], -jnp.inf, a)
        a = jax.nn.softmax(a, axis=-1)
        a = jnp.nan_to_num(a)
        o = jnp.einsum('bhnm,bmhd->bnhd', a, v).reshape(B, N, HIDDEN)
        return o @ Wo.T + bo

    def _L0_ffn_ref(x, router_w, router_b, w1, b1, w2, b2, ln_g, ln_b):
        import jax, jax.numpy as jnp
        import numpy as np
        B, L, D, E, TOP_K = (8, 512, 384, 4, 2)
        H = 2 * D
        LN_EPS = 1e-05

        def _gelu(v):
            return jax.nn.gelu(v, approximate=False)

        def _mish(v):
            return v * jnp.tanh(jax.nn.softplus(v))
        _ACTS = [_gelu, jax.nn.silu, _mish, _gelu]
        b, l, d = x.shape
        e = router_w.shape[0]
        pooled = x.mean(axis=1)
        logits = pooled @ router_w.T + router_b
        top_v, top_i = jax.lax.top_k(logits, TOP_K)
        gates_k = jax.nn.softmax(top_v, axis=-1)
        gate = jnp.zeros((b, e), x.dtype).at[jnp.arange(b)[:, None], top_i].add(gates_k)
        h = jnp.einsum('bld,edh->belh', x, w1) + b1[None, :, None, :]
        h = jnp.stack([_ACTS[i](h[:, i]) for i in range(e)], axis=1)
        out = jnp.einsum('belh,ehd->beld', h, w2) + b2[None, :, None, :]
        y = jnp.einsum('be,beld->bld', gate, out) + x
        mu = y.mean(axis=-1, keepdims=True)
        var = ((y - mu) ** 2).mean(axis=-1, keepdims=True)
        return (y - mu) * jax.lax.rsqrt(var + LN_EPS) * ln_g + ln_b
    x = x + _L0_gnn_ref(_layernorm(x, axis=-1), adj, L0_gnn_Wq, L0_gnn_Wk, L0_gnn_Wv, L0_gnn_bv, L0_gnn_Wo, L0_gnn_bo)
    x = x + _L0_ffn_ref(_layernorm(x, axis=-1), L0_ffn_router_w, L0_ffn_router_b, L0_ffn_w1, L0_ffn_b1, L0_ffn_w2, L0_ffn_b2, L0_ffn_ln_g, L0_ffn_ln_b)
    return x

_drawn_inputs = setup_inputs


def setup_inputs(seed=0):
    import zlib

    import numpy as np

    out = dict(_drawn_inputs(seed))
    spreads = {'L0_ffn_router_b': (0.0, 0.1), 'L0_ffn_ln_g': (1.0, 0.2), 'L0_ffn_ln_b': (0.0, 0.1)}
    factors = {'L0_ffn_b1': 24.802, 'L0_ffn_b2': 8.0}
    for name, (base, spread) in spreads.items():
        noise = np.random.default_rng([zlib.crc32(name.encode()), seed]).standard_normal(out[name].shape)
        drawn = base * np.exp(spread * noise) if base else spread * noise
        out[name] = jnp.asarray(drawn.astype(out[name].dtype))
    for name, factor in factors.items():
        out[name] = (out[name] * factor).astype(out[name].dtype)
    return out
```

```python
from contextlib import ExitStack

import concourse.bass as bass
from concourse import mybir

F32 = mybir.dt.float32
F32R = mybir.dt.float32r
I32 = mybir.dt.int32
F16 = mybir.dt.float16
BF16 = mybir.dt.bfloat16
ALU = mybir.AluOpType
ACT = mybir.ActivationFunctionType
AX = mybir.AxisListType

P = 128
BANK = 512
EPS = 1e-5
LOWEST = -3.4028234e38


def reached(engine, semaphore, count):
    if not isinstance(count, int) or count > 0:
        engine.wait_ge(semaphore, count)


def gnn_moe_kernel(nc, x, adj, Wq, Wk, Wv, bv, Wo, bo, router_w, router_b, w1, b1, w2, b2, ln_g, ln_b, out):
    B, N, D = x.shape
    E, _, F = w1.shape
    HEAD = 32
    HEADS = D // HEAD
    DC = D // P
    FC = F // P
    QUAD = P // HEAD
    PAIRS = B // 2
    K = 2
    SCALE = float(D) ** -0.5
    VW = HEAD + 1
    PTC = HEADS * N // BANK
    HPB = BANK // N
    HALF = F // 2
    assert N == P and D % P == 0 and F % P == 0 and HALF <= BANK and B % 4 == 0 and QUAD * DC == HEADS

    x1_dram = nc.dram_tensor("x1_scratch", (B, N, D), F32, kind="Internal").ap()

    with ExitStack() as ctx:
        def sb(name, shape, dt=F32, to=ctx):
            return to.enter_context(nc.sbuf_tensor(name, shape, dt))

        def ps(name, shape, dt=F32):
            return ctx.enter_context(nc.psum_tensor(name, shape, dt))

        def sem(name):
            return ctx.enter_context(nc.semaphore(name))

        ident = sb("ident", [P, P])
        mean_w = sb("mean_w", [P, 1])
        half_col = sb("half_col", [P, 1])
        neg_half = sb("neg_half", [P, 2])
        pooled = sb("pooled", [P, B, DC])
        gate = sb("gate", [P, B, K])
        expert = sb("expert", [P, B, K], I32)

        s1 = ExitStack()
        wt_hi = [sb(f"wt_hi{m}", [P, DC, D], F32R, s1) for m in range(4)]
        wt_lo = [sb(f"wt_lo{m}", [P, DC, D], F32R, s1) for m in range(4)]
        w_raw = [sb(f"w_raw{m}", [P, DC, D], F32, s1) for m in range(4)]
        rw_t = sb("rw_t", [P, DC, E], F32, s1)
        rw_wide = sb("rw_wide", [P, DC, E, P], F32, s1)
        rb_wide = sb("rb_wide", [P, E], F32, s1)
        bv_wide = sb("bv_wide", [P, D], F32, s1)
        bo_wide = sb("bo_wide", [P, D], F32, s1)
        x_in = [sb(f"x_in{p}", [P, 2, D], F32, s1) for p in range(2)]
        adj_in = [sb(f"adj_in{p}", [P, 2, N], F32, s1) for p in range(2)]
        x1_sb = [sb(f"x1_sb{p}", [P, 2, D], F32, s1) for p in range(2)]
        xn = sb("xn", [P, 2, D], F32, s1)
        xt_hi = sb("xt_hi", [P, DC, 2 * N], F32R, s1)
        xt_lo = sb("xt_lo", [P, DC, 2 * N], F32R, s1)
        q_t = [sb(f"q_t{p}", [P, DC, 2 * N], F32, s1) for p in range(2)]
        k_t = [sb(f"k_t{p}", [P, DC, 2 * N], F32, s1) for p in range(2)]
        v_sum = [sb(f"v_sum{g}", [P, D], F32, s1) for g in range(2)]
        v_hi = [sb(f"v_hi{p}", [P, 2, HEADS, VW], BF16, s1) for p in range(2)]
        v_mid = [sb(f"v_mid{p}", [P, 2, HEADS, VW], BF16, s1) for p in range(2)]
        v_lo = [sb(f"v_lo{p}", [P, 2, HEADS, VW], BF16, s1) for p in range(2)]
        att = [sb(f"att{g}", [P, HEADS, N], F32, s1) for g in range(2)]
        prob = [sb(f"prob{g}", [P, HEADS, N], F32, s1) for g in range(2)]
        pt_hi = [sb(f"pt_hi{c}", [P, BANK], F16, s1) for c in range(PTC)]
        pt_lo = [sb(f"pt_lo{c}", [P, BANK], F16, s1) for c in range(PTC)]
        o_sb = [sb(f"o_sb{g}", [P, D], F32, s1) for g in range(2)]
        ot_hi = [sb(f"ot_hi{g}", [P, DC, N], F32R, s1) for g in range(2)]
        ot_lo = [sb(f"ot_lo{g}", [P, DC, N], F32R, s1) for g in range(2)]
        u_att = sb("u_att", [P, 2, D], F32, s1)
        fold = sb("fold", [P, HEADS, N // 2], F32, s1)
        row_max = [sb(f"row_max{g}", [P, HEADS], F32, s1) for g in range(2)]
        neg_max = [sb(f"neg_max{g}", [P, HEADS], F32, s1) for g in range(2)]
        keep = [sb(f"keep{g}", [P, HEADS], F32, s1) for g in range(2)]
        zero_max = sb("zero_max", [P, HEADS], F32, s1)
        zero_sum = sb("zero_sum", [P, HEADS], F32, s1)
        inv_sum = [sb(f"inv_sum{g}", [P, HEADS], F32, s1) for g in range(2)]
        inv_kept = [sb(f"inv_kept{g}", [P, HEADS], F32, s1) for g in range(2)]
        st1 = sb("st1", [P, 2, 6], F32, s1)
        mv1 = sb("mv1", [P, 2, 2], F32, s1)
        rs1 = sb("rs1", [P, 2], F32, s1)
        st2 = sb("st2", [P, 2, 6], F32, s1)
        mv2 = sb("mv2", [P, 2, 2], F32, s1)
        rs2 = sb("rs2", [P, 2], F32, s1)
        e_wide = sb("e_wide", [P, E], F32, s1)
        e_less = sb("e_less", [P, E], F32, s1)
        logit = sb("logit", [P, B, E], F32, s1)
        hit = sb("hit", [P, B, E], F32, s1)
        top = sb("top", [P, K, B], F32, s1)
        top_e = sb("top_e", [P, K, B], F32, s1)
        g_tmp = sb("g_tmp", [P, 3, B], F32, s1)
        s1.close()

        w1_hi = sb("w1_hi", [P, E, DC, F], F32R)
        w1_lo = sb("w1_lo", [P, E, DC, F], F32R)
        w2_hi = sb("w2_hi", [P, E, FC, D], F32R)
        w2_lo = sb("w2_lo", [P, E, FC, D], F32R)
        b1_wide = sb("b1_wide", [P, E, 2, HALF])
        b2_wide = sb("b2_wide", [P, E, D])
        lng_wide = sb("lng_wide", [P, D])
        lnb_wide = sb("lnb_wide", [P, D])
        x1_in = [sb(f"x1_in{m}", [P, D]) for m in range(4)]
        z_sb = [sb(f"z_sb{m}", [P, D]) for m in range(4)]
        ut_hi = sb("ut_hi", [P, DC, N], F32R)
        ut_lo = sb("ut_lo", [P, DC, N], F32R)
        st_u = sb("st_u", [P, 6])
        mv_u = sb("mv_u", [P, 2])
        rs_u = sb("rs_u", [P, 1])
        st_z = sb("st_z", [P, 6])
        mv_z = sb("mv_z", [P, 2])
        rs_z = sb("rs_z", [P, 1])
        gate_col = sb("gate_col", [P, 4])
        stage = ExitStack()
        w_stage = [sb(f"w_stage{m}", [P, DC * F], F32, stage) for m in range(2)]
        stage.close()
        bias_part = [sb(f"bias_part{k}", [P, D]) for k in range(K)]
        hid = [sb(f"hid{k}", [P, 2, HALF]) for k in range(K)]
        half_t = sb("half_t", [P, 2, HALF])
        denom = sb("denom", [P, 2, HALF])
        at_hi = sb("at_hi", [P, FC, N], F32R)
        at_lo = sb("at_lo", [P, FC, N], F32R)
        out_sb = [sb(f"out_sb{m}", [P, D]) for m in range(2)]

        score = [ps(f"score{r}", [P, BANK]) for r in range(4)]
        slot = [ps(f"slot{r}", [P, BANK]) for r in range(4)]

        passed = sem("passed")

        def reached_before(engine, semaphore, count):
            reached(engine, semaphore, count)
            if not isinstance(count, int):
                engine.sem_inc(passed, 1)

        const_ready = sem("const_ready")
        small_loaded = sem("small_loaded")
        w_loaded = [sem(f"w_loaded{m}") for m in range(4)]
        ident_ready = sem("ident_ready")
        wt_mm, wt_hi_done, wt_lo_done = sem("wt_mm"), sem("wt_hi_done"), sem("wt_lo_done")
        x_loaded = [sem(f"x_loaded{p}") for p in range(2)]
        adj_loaded = [sem(f"adj_loaded{p}") for p in range(2)]
        x1_stored = [sem(f"x1_stored{p}") for p in range(2)]
        st1_done, mv1_ready, rs1_eps, rs1_ready = sem("st1_done"), sem("mv1_ready"), sem("rs1_eps"), sem("rs1_ready")
        xn_ready = sem("xn_ready")
        xt_mm, xt_hi_done, xt_lo_done = sem("xt_mm"), sem("xt_hi_done"), sem("xt_lo_done")
        q_mm, q_done = sem("q_mm"), sem("q_done")
        k_mm, k_done = sem("k_mm"), sem("k_done")
        v_mm, v_done = sem("v_mm"), sem("v_done")
        v_hi_done, v_rest_done, v_mid_done, v_split = sem("v_hi_done"), sem("v_rest_done"), sem("v_mid_done"), sem("v_split")
        s_mm, max_ready, neg_ready = sem("s_mm"), sem("max_ready"), sem("neg_ready")
        exp_done = sem("exp_done")
        fold_done, zero_done, keep_ready = sem("fold_done"), sem("zero_done"), sem("keep_ready")
        pt_mm, pt_hi_done, pt_done = sem("pt_mm"), sem("pt_hi_done"), sem("pt_done")
        o_mm, inv_done, kept_done, o_done = sem("o_mm"), sem("inv_done"), sem("kept_done"), sem("o_done")
        ot_mm, ot_hi_done, ot_lo_done = sem("ot_mm"), sem("ot_hi_done"), sem("ot_lo_done")
        wo_mm, xbo_ready, x1_done = sem("wo_mm"), sem("xbo_ready"), sem("x1_done")
        st2_done, mv2_ready, rs2_eps, rs2_ready = sem("st2_done"), sem("mv2_ready"), sem("rs2_eps"), sem("rs2_ready")
        u_ready, pooled_mm, pooled_done = sem("u_ready"), sem("pooled_mm"), sem("pooled_done")
        logit_mm, route_step, route_exp, routed = sem("logit_mm"), sem("route_step"), sem("route_exp"), sem("routed")
        stage_loaded = [sem(f"stage_loaded{m}") for m in range(2)]
        wide_loaded = sem("wide_loaded")
        split_hi, split_lo = sem("split_hi"), sem("split_lo")
        x1_loaded = [sem(f"x1_loaded{m}") for m in range(4)]
        out_stored = [sem(f"out_stored{m}") for m in range(2)]
        st_u_done, mv_u_ready, rs_u_eps, rs_u_ready = sem("st_u_done"), sem("mv_u_ready"), sem("rs_u_eps"), sem("rs_u_ready")
        st_z_done, mv_z_ready, rs_z_eps, rs_z_ready = sem("st_z_done"), sem("mv_z_ready"), sem("rs_z_eps"), sem("rs_z_ready")
        un_ready, ut_mm, ut_hi_done, ut_lo_done = sem("un_ready"), sem("ut_mm"), sem("ut_hi_done"), sem("ut_lo_done")
        h_mm, hid_done = sem("h_mm"), sem("hid_done")
        tanh_done, square_done, act_done, mish_step = sem("tanh_done"), sem("square_done"), sem("act_done"), sem("mish_step")
        a_ready = [sem(f"a_ready{k}") for k in range(K)]
        at_mm, at_hi_done, at_lo_done = sem("at_mm"), sem("at_hi_done"), sem("at_lo_done")
        gate_copied, y_mm = sem("gate_copied"), sem("y_mm")
        bias_scaled, bias_half, z_added, zn_done = sem("bias_scaled"), sem("bias_half"), sem("z_added"), sem("zn_done")
        zg_done, zx_done, out_ready = sem("zg_done"), sem("zx_done"), sem("out_ready")

        block = ctx.enter_context(nc.Block())

        def attention_steps(engine, step):
            for t in range(-2, 2):
                step(t, t % 2, t // 2)
            with engine.Fori(1, PAIRS // 2 - 1) as i:
                for p in range(2):
                    step(i * 2 + p, p, i)
            for t in range(PAIRS - 2, PAIRS + 1):
                step(t, t % 2, t // 2)

        def has(t, ahead):
            return not isinstance(t, int) or 0 <= t + ahead < PAIRS

        def expert_steps(engine, step):
            for b in range(-1, 4):
                step(b, b % 4, b // 4)
            with engine.Fori(1, B // 4 - 1) as i:
                for m in range(4):
                    step(i * 4 + m, m, i)
            for b in range(B - 4, B + 2):
                step(b, b % 4, b // 4)

        def heads(v):
            return v[:].rearrange("p (h d) -> p h d", h=HEADS)

        def graph(b, ahead):
            return not isinstance(b, int) or 0 <= b + ahead < B

        @block.sync
        def _(sp):
            for m, w in enumerate((Wq, Wk, Wv, Wo)):
                sp.dma_start(w_raw[m][:], w.rearrange("(c p) d -> p c d", p=P)).then_inc(w_loaded[m], 16)
                if m < 2:
                    sp.dma_start(x_in[m][:], x[2 * m:2 * m + 2].rearrange("g n d -> n g d")).then_inc(x_loaded[m], 16)
                    sp.dma_start(adj_in[m][:], adj[2 * m:2 * m + 2].rearrange("g n d -> n g d")).then_inc(adj_loaded[m], 16)
            sp.dma_start(bv_wide[:], bv.rearrange("(o d) -> o d", o=1).partition_broadcast(P)).then_inc(small_loaded, 16)
            sp.dma_start(bo_wide[:], bo.rearrange("(o d) -> o d", o=1).partition_broadcast(P)).then_inc(small_loaded, 16)
            sp.dma_start(rb_wide[:], router_b.rearrange("(o d) -> o d", o=1).partition_broadcast(P)).then_inc(small_loaded, 16)
            for c in range(DC):
                sp.dma_start(rw_t[:, c, :], router_w[:, c * P:(c + 1) * P].rearrange("e p -> p e"), allow_slow_non_contiguous=True).then_inc(small_loaded, 16)

            def step(t, p, lap):
                if has(t, 0) and has(t, 2):
                    reached(sp, xbo_ready, t + 1)
                    reached(sp, xn_ready, t + 1)
                    sp.dma_start(x_in[p][:], x[pair(t, 2)].rearrange("g n d -> n g d")).then_inc(x_loaded[p], 16)
                if has(t, -1):
                    reached(sp, x1_done, 2 * t)
                    sp.dma_start(x1_dram[pair(t, -1)].rearrange("g n d -> n g d"), x1_sb[1 - p][:]).then_inc(x1_stored[1 - p], 16)
                if has(t, 0) and has(t, 2):
                    reached(sp, neg_ready, 8 * (t + 1))
                    sp.dma_start(adj_in[p][:], adj[pair(t, 2)].rearrange("g n d -> n g d")).then_inc(adj_loaded[p], 16)

            def pair(t, ahead):
                return slice(2 * (t + ahead), 2 * (t + ahead) + 2) if isinstance(t, int) else bass.ds(t * 2 + 2 * ahead, 2)

            attention_steps(sp, step)

            for p in range(2):
                sp.wait_ge(x1_stored[p], 16 * (PAIRS // 2))
            sp.wait_ge(routed, 1)
            for m in range(4):
                sp.dma_start(x1_in[m][:], x1_dram[m]).then_inc(x1_loaded[m], 16)
            for m in range(2 * E):
                if m >= 2:
                    sp.wait_ge(split_lo, m - 1)
                src = w1[m].rearrange("(c p) f -> p c f", p=P) if m < E else w2[m - E].rearrange("(c p) d -> p c d", p=P)
                c = DC if m < E else FC
                sp.dma_start(w_stage[m % 2][:].rearrange("p (c f) -> p c f", c=c), src).then_inc(stage_loaded[m % 2], 16)
                if m == 0:
                    sp.dma_start(b1_wide[:].rearrange("p e s f -> p (e s f)"), b1.rearrange("(o e) f -> o (e f)", o=1).partition_broadcast(P)).then_inc(wide_loaded, 16)
                    sp.dma_start(b2_wide[:].rearrange("p e d -> p (e d)"), b2.rearrange("(o e) d -> o (e d)", o=1).partition_broadcast(P)).then_inc(wide_loaded, 16)
                    sp.dma_start(lng_wide[:], ln_g.rearrange("(o d) -> o d", o=1).partition_broadcast(P)).then_inc(wide_loaded, 16)
                    sp.dma_start(lnb_wide[:], ln_b.rearrange("(o d) -> o d", o=1).partition_broadcast(P)).then_inc(wide_loaded, 16)

            def finish(b, m):
                reached(sp, out_ready, b + 1)
                sp.dma_start(one(out, b, 0), out_sb[m % 2][:]).then_inc(out_stored[m % 2], 16)
                if graph(b, 4):
                    sp.dma_start(x1_in[m][:], one(x1_dram, b, 4)).then_inc(x1_loaded[m], 16)

            def one(tensor, b, ahead):
                return tensor[b + ahead] if isinstance(b, int) else tensor[bass.ds(b + ahead, 1)].rearrange("o n d -> (o n) d")

            with sp.Fori(0, B // 4 - 1) as i:
                for m in range(4):
                    sp.wait_ge(out_ready, i * 4 + m + 1)
                    sp.dma_start(one(out, i * 4 + m, 0), out_sb[m % 2][:]).then_inc(out_stored[m % 2], 16)
                    sp.dma_start(x1_in[m][:], one(x1_dram, i * 4 + m, 4)).then_inc(x1_loaded[m], 16)
            for b in range(B - 4, B):
                finish(b, b % 4)
            for m in range(2):
                sp.wait_ge(out_stored[m], 16 * (B // 2))

        @block.tensor
        def _(pe):
            def split_product(acc, lhs, rhs, start=True, stop=True):
                terms = [(a, b, c) for c in range(len(lhs)) for a, b in ((0, 0), (0, 1), (1, 0))]
                for n, (a, b, c) in enumerate(terms):
                    last = nc.tensor.matmul(acc, lhs[c][a], rhs[c][b], start=start and n == 0,
                                            stop=stop and n == len(terms) - 1)
                return last

            pe.wait_ge(ident_ready, 2)
            for m in range(4):
                pe.wait_ge(w_loaded[m], 16)
                for dc in range(DC):
                    n = m * DC + dc
                    if n >= 4:
                        pe.wait_ge(wt_lo_done, n - 3)
                    for oc in range(DC):
                        last = nc.tensor.transpose(slot[n % 4][:, oc * P:(oc + 1) * P],
                                                   w_raw[m][:, oc, dc * P:(dc + 1) * P], ident[:])
                    last.then_inc(wt_mm, 1)

            def project_t(dst, m, oc):
                return split_product(dst, [(wt_hi[m][:, c, oc * P:(oc + 1) * P], wt_lo[m][:, c, oc * P:(oc + 1) * P]) for c in range(DC)],
                                     [(xt_hi[:, c, :], xt_lo[:, c, :]) for c in range(DC)])

            def project_two(m, first, second, done):
                for oc in range(DC):
                    bank = first if oc < 2 else second
                    last = project_t(bank[:, (oc % 2) * 2 * N:(oc % 2 + 1) * 2 * N], m, oc)
                    if oc > 0:
                        last.then_inc(done, 1)

            def project_v(dst, g):
                split_product(dst[:, 0:D], [(xt_hi[:, c, g * N:(g + 1) * N], xt_lo[:, c, g * N:(g + 1) * N]) for c in range(DC)],
                              [(wt_hi[2][:, c, :], wt_lo[2][:, c, :]) for c in range(DC)]).then_inc(v_mm, 1)

            def scores(t, p, g):
                for r in range(QUAD):
                    reached(pe, neg_ready, 4 * (2 * t + g - 1) + r + 1)
                    for c in range(DC):
                        rows = slice(HEAD * r, HEAD * (r + 1))
                        last = nc.tensor.matmul(score[r][:, c * N:(c + 1) * N], q_t[p][rows, c, g * N:(g + 1) * N],
                                                k_t[p][rows, c, g * N:(g + 1) * N], start=True, stop=True)
                    last.then_inc(s_mm, 1)

            def transpose_probs(t, g, c, bank):
                reached(pe, exp_done, HEADS * (2 * t + g) + HPB * (c + 1))
                for i in range(HPB):
                    last = nc.tensor.transpose(bank[:, i * N:(i + 1) * N], prob[g][:, c * HPB + i, :], ident[:])
                last.then_inc(pt_mm, 1)

            def attend(t, p, g, bank):
                reached(pe, pt_done, PTC * (2 * t + g) + PTC)
                reached(pe, v_split, 2 * t + g + 1)
                for hh in range(HEADS):
                    h = QUAD * (hh % DC) + hh // DC
                    cols = slice((hh % HPB) * N, (hh % HPB + 1) * N)
                    hi, lo = pt_hi[hh // HPB][:, cols], pt_lo[hh // HPB][:, cols]
                    terms = [(hi, v_hi), (hi, v_mid), (hi, v_lo), (lo, v_hi), (lo, v_mid)]
                    for n, (pt, v) in enumerate(terms):
                        last = nc.tensor.matmul(bank[:, hh * VW:(hh + 1) * VW], pt, v[p][:, g, h, :],
                                                start=n == 0, stop=n == len(terms) - 1)
                last.then_inc(o_mm, 1)

            def transpose_o(t, g, bank):
                reached(pe, o_done, 2 * t + g + 1)
                for c in range(DC):
                    last = nc.tensor.transpose(bank[:, c * N:(c + 1) * N], o_sb[g][:, c * P:(c + 1) * P], ident[:])
                last.then_inc(ot_mm, 1)

            def project_o(t, g, bank):
                reached(pe, ot_lo_done, 2 * t + g + 1)
                split_product(bank[:, 0:D], [(ot_hi[g][:, c, :], ot_lo[g][:, c, :]) for c in range(DC)],
                              [(wt_hi[3][:, c, :], wt_lo[3][:, c, :]) for c in range(DC)]).then_inc(wo_mm, 1)

            def step(t, p, lap):
                now, nxt, prev = has(t, 0), has(t, 1), has(t, -1)
                if isinstance(t, int) and t == -1:
                    pe.wait_ge(wt_lo_done, 4 * DC)
                if isinstance(t, int) and t == 0:
                    pe.wait_ge(q_done, 2)
                    pe.wait_ge(k_done, 2)
                    pe.wait_ge(v_done, 2)
                if nxt:
                    reached(pe, xn_ready, t + 2)
                    if prev:
                        pe.wait_ge(ot_lo_done, 2 * t - 1)
                        pe.wait_ge(o_done, 2 * t)
                    for c in range(DC):
                        for g in range(2):
                            last = nc.tensor.transpose(slot[c // 2][:, ((c % 2) * 2 + g) * N:((c % 2) * 2 + g + 1) * N],
                                                       xn[:, g, c * P:(c + 1) * P], ident[:])
                        if c > 0:
                            last.then_inc(xt_mm, 1)
                if now:
                    reached(pe, q_done, 2 * (t + 1))
                    reached(pe, k_done, 2 * (t + 1))
                    scores(t, p, 0)
                if prev:
                    reached(pe, x1_done, 2 * t - 1)
                    project_o(t - 1, 1, slot[2])
                if nxt:
                    reached(pe, xt_lo_done, 2 * (t + 2))
                    reached(pe, ot_lo_done, 2 * t)
                    project_two(0, slot[3], slot[0], q_mm)
                if now:
                    scores(t, p, 1)
                if prev:
                    reached(pe, x1_done, 2 * t)
                if nxt:
                    project_two(1, slot[1], slot[2], k_mm)
                if now:
                    if nxt:
                        reached(pe, q_done, 2 * (t + 1) + 2)
                    else:
                        reached(pe, ot_lo_done, 2 * t)
                    transpose_probs(t, 0, 0, slot[3])
                    transpose_probs(t, 0, 1, slot[0])
                    if nxt:
                        reached(pe, k_done, 2 * (t + 1) + 1)
                    else:
                        reached(pe, o_done, 2 * t)
                    transpose_probs(t, 0, 2, slot[1])
                if nxt:
                    reached(pe, k_done, 2 * (t + 1) + 2)
                if prev:
                    reached(pe, u_ready, 2 * t)
                    for g in range(2):
                        for c in range(DC):
                            last = nc.tensor.matmul(slot[2][:, D + g * DC + c:D + g * DC + c + 1],
                                                    u_att[:, g, c * P:(c + 1) * P], mean_w[:], start=True, stop=True)
                    last.then_inc(pooled_mm, 1)
                if nxt:
                    project_v(slot[2], 0)
                if now:
                    attend(t, p, 0, slot[3])
                    transpose_probs(t, 1, 0, slot[0])
                    transpose_probs(t, 1, 1, slot[1])
                    if nxt:
                        reached(pe, v_done, 2 * (t + 1) + 1)
                    if prev:
                        reached(pe, pooled_done, t)
                    transpose_probs(t, 1, 2, slot[2])
                    reached(pe, o_done, 2 * t + 1)
                elif nxt:
                    reached(pe, q_done, 2 * (t + 1) + 1)
                if nxt:
                    project_v(slot[3], 1)
                if now:
                    reached(pe, pt_done, PTC * (2 * t + 1) + 1)
                    transpose_o(t, 0, slot[0])
                    attend(t, p, 1, slot[1])
                    project_o(t, 0, slot[2])
                    if nxt:
                        reached(pe, v_done, 2 * (t + 1) + 2)
                    transpose_o(t, 1, slot[3])

            attention_steps(pe, step)

            pe.wait_ge(pooled_done, PAIRS)
            for e in range(E):
                for c in range(DC):
                    last = nc.tensor.matmul(slot[0][:, e * B:(e + 1) * B], rw_wide[:, c, e, :], pooled[:, :, c],
                                            start=c == 0, stop=c == DC - 1)
            last.then_inc(logit_mm, 1)
            pe.wait_ge(routed, 1)

            hid_ps, at_ps, y_ps, ut_ps = score[0:2], score[2:4], slot[0:2], slot[2]

            def choice(b, k):
                i = b * K + k
                cell = expert[0:1].rearrange("p b k -> p (b k)")
                cell = cell[:, i:i + 1] if isinstance(i, int) else cell[:, bass.ds(i, 1)]
                return pe.value_load(cell, min_val=0, max_val=E - 1)

            def transpose_act(b, k):
                i = b * K + k
                reached(pe, a_ready[k], b + 1)
                reached(pe, at_lo_done, i)
                for c in range(FC):
                    last = nc.tensor.transpose(at_ps[c // DC][:, (c % DC) * P:(c % DC + 1) * P],
                                               hid[k][:, c // DC, (c % DC) * P:(c % DC + 1) * P], ident[:])
                last.then_inc(at_mm, 1)

            def first_layer(b, k):
                i = b * K + k
                e = choice(b, k)
                reached(pe, ut_lo_done, b + 1)
                reached(pe, hid_done, i)
                for s in range(2):
                    last = split_product(hid_ps[s][:, 0:HALF], [(ut_hi[:, c, :], ut_lo[:, c, :]) for c in range(DC)],
                                         [tuple(w[:].rearrange("p e c f -> p (e c f)")[:, bass.ds(e * (DC * F) + (c * F + s * HALF), HALF)]
                                                for w in (w1_hi, w1_lo)) for c in range(DC)])
                last.then_inc(h_mm, 1)

            def second_layer(b, k, m):
                i = b * K + k
                e = choice(b, k)
                if k == 0:
                    reached(pe, z_added, b - 1)
                reached(pe, at_lo_done, i + 1)
                split_product(y_ps[m % 2][:, 0:D], [(at_hi[:, c, :], at_lo[:, c, :]) for c in range(FC)],
                              [tuple(w[:].rearrange("p e c d -> p (e c d)")[:, bass.ds(e * (FC * D) + c * D, D)]
                                     for w in (w2_hi, w2_lo)) for c in range(FC)],
                              start=k == 0, stop=k == K - 1).then_inc(y_mm, 1)

            def expert_step(b, m, lap):
                for k in range(K):
                    if graph(b, -1):
                        transpose_act(b - 1, k)
                    if graph(b, 0):
                        if isinstance(b, int) and b == 0 and k == 0:
                            pe.wait_ge(split_lo, E)
                        first_layer(b, k)
                    if k == 1 and graph(b, 1):
                        reached(pe, un_ready, b + 2)
                        reached(pe, ut_lo_done, b + 1)
                        for c in range(DC):
                            last = nc.tensor.transpose(ut_ps[:, c * N:(c + 1) * N], z_sb[(m + 1) % 4][:, c * P:(c + 1) * P], ident[:])
                        last.then_inc(ut_mm, 1)
                    if graph(b, -1):
                        if isinstance(b, int) and b == 1 and k == 0:
                            pe.wait_ge(split_lo, 2 * E)
                        second_layer(b - 1, k, m - 1)

            expert_steps(pe, expert_step)

        @block.scalar
        def _(act):
            for n in range(4 * DC):
                act.wait_ge(wt_mm, n + 1)
                nc.scalar.activation(wt_hi[n // DC][:, n % DC, :], slot[n % 4][:, 0:D], ACT.Copy).then_inc(wt_hi_done, 1)

            def exps(t, g):
                for r in range(QUAD):
                    reached(act, neg_ready, 4 * (2 * t + g) + r + 1)
                    for c in range(DC):
                        hh = r * DC + c
                        nc.scalar.activation(prob[g][:, hh, :], att[g][:, hh, :], ACT.Exp,
                                             bias=neg_max[g][:, hh:hh + 1]).then_inc(exp_done, 1)

            def step(t, p, lap):
                now, nxt = has(t, 0), has(t, 1)
                if nxt:
                    reached(act, xt_mm, 2 * (t + 1) + 1)
                    nc.scalar.activation(xt_hi[:, 0:2, :], slot[0][:].rearrange("p (c n) -> p c n", c=2), ACT.Copy).then_inc(xt_hi_done, 1)
                    reached(act, xt_mm, 2 * (t + 1) + 2)
                    nc.scalar.activation(xt_hi[:, 2, :], slot[1][:, 0:2 * N], ACT.Copy).then_inc(xt_hi_done, 1)
                if now:
                    for g in range(2):
                        reached(act, v_done, 2 * t + g + 1)
                        nc.scalar.activation(v_hi[p][:, g, :, 0:HEAD], heads(v_sum[g]), ACT.Copy).then_inc(v_hi_done, 1)
                    for g in range(2):
                        reached(act, v_rest_done, 2 * t + g + 1)
                        nc.scalar.activation(v_mid[p][:, g, :, 0:HEAD], heads(v_sum[g]), ACT.Copy).then_inc(v_mid_done, 1)
                    exps(t, 0)
                if nxt:
                    reached(act, q_mm, 2 * (t + 1) + 1)
                    nc.scalar.activation(q_t[1 - p][:, 0:2, :], slot[3][:].rearrange("p (c n) -> p c n", c=2), ACT.Copy, scale=SCALE).then_inc(q_done, 1)
                    reached(act, q_mm, 2 * (t + 1) + 2)
                    nc.scalar.activation(q_t[1 - p][:, 2, :], slot[0][:, 0:2 * N], ACT.Copy, scale=SCALE).then_inc(q_done, 1)
                if now:
                    exps(t, 1)
                    for g in range(2):
                        for c in range(PTC):
                            bank = slot[(3, 0, 1)[c]] if g == 0 else slot[c]
                            reached(act, pt_mm, PTC * (2 * t + g) + c + 1)
                            nc.scalar.activation(pt_hi[c][:], bank[:], ACT.Copy).then_inc(pt_hi_done, 1)
                    for g in range(2):
                        reached(act, ot_mm, 2 * t + g + 1)
                        nc.scalar.activation(ot_hi[g][:].rearrange("p c n -> p (c n)"), slot[3 * g][:, 0:D], ACT.Copy).then_inc(ot_hi_done, 1)

            attention_steps(act, step)

            act.wait_ge(route_exp, 1)
            nc.scalar.activation(g_tmp[:, 1, :], g_tmp[:, 0, :], ACT.Exp).then_inc(route_exp, 1)
            act.wait_ge(routed, 1)

            for m in range(2 * E):
                hi = w1_hi[:, m].rearrange("p c f -> p (c f)") if m < E else w2_hi[:, m - E].rearrange("p c d -> p (c d)")
                act.wait_ge(stage_loaded[m % 2], 16 * (m // 2 + 1))
                nc.scalar.activation(hi, w_stage[m % 2][:], ACT.Copy).then_inc(split_hi, 1)
                if m == 1:
                    act.wait_ge(ut_mm, 1)
                    nc.scalar.activation(ut_hi[:].rearrange("p c n -> p (c n)"), slot[2][:, 0:D], ACT.Copy).then_inc(ut_hi_done, 1)

            nc.scalar.preload_act_table(ACT.Gelu)
            at_ps, ut_ps = score[2:4], slot[2]

            def choice(b, k):
                i = b * K + k
                cell = expert[0:1].rearrange("p b k -> p (b k)")
                cell = cell[:, i:i + 1] if isinstance(i, int) else cell[:, bass.ds(i, 1)]
                return act.value_load(cell, min_val=0, max_val=E - 1)

            def split_act_hi(b, k, m):
                i = b * K + k
                reached(act, at_mm, i + 1)
                col = (m * K + k) % 4
                for s in range(2):
                    last = nc.scalar.activation(at_hi[:, s * DC:(s + 1) * DC, :].rearrange("p c n -> p (c n)"), at_ps[s][:, 0:HALF],
                                                ACT.Copy, scale=gate_col[:, col:col + 1])
                last.then_inc(at_hi_done, 1)

            def activate(b, k):
                i = b * K + k
                reached(act, hid_done, i + 1)
                e = choice(b, k)
                with act.If(e == 1):
                    for s in range(2):
                        nc.scalar.activation(half_t[:, s], hid[k][:, s], ACT.Tanh, scale=0.5).then_inc(tanh_done, 1)
                    for s in range(2):
                        act.wait_ge(tanh_done, 2 * i + s + 1)
                        nc.scalar.activation(half_t[:, s], half_t[:, s], ACT.Copy, scale=0.5, bias=0.5).then_inc(act_done, 1)
                    act.sem_inc(square_done, 2)
                with act.Else():
                    with act.If(e == 2):
                        for s in range(2):
                            nc.scalar.activation(half_t[:, s], hid[k][:, s], ACT.Tanh, scale=0.5).then_inc(tanh_done, 1)
                        for s in range(2):
                            act.wait_ge(tanh_done, 2 * i + s + 1)
                            nc.scalar.activation(half_t[:, s], half_t[:, s], ACT.Square, scale=-0.5, bias=half_col[:]).then_inc(square_done, 1)
                        for s in range(2):
                            act.wait_ge(square_done, 2 * i + s + 1)
                            nc.scalar.activation(denom[:, s], half_t[:, s], ACT.Copy, bias=1.0).then_inc(act_done, 1)
                    with act.Else():
                        nc.scalar.activation(hid[k][:], hid[k][:], ACT.Gelu).then_inc(a_ready[k], 1)
                        act.sem_inc(tanh_done, 2)
                        act.sem_inc(square_done, 2)
                        act.sem_inc(act_done, 2)

            def expert_step(b, m, lap):
                for k in range(K):
                    if graph(b, -1):
                        split_act_hi(b - 1, k, m - 1)
                    if k == 1 and graph(b, 1) and not (isinstance(b, int) and b == -1):
                        reached(act, ut_mm, b + 2)
                        nc.scalar.activation(ut_hi[:].rearrange("p c n -> p (c n)"), ut_ps[:, 0:D], ACT.Copy).then_inc(ut_hi_done, 1)
                    if graph(b, 0):
                        activate(b, k)
                        scale_output_bias(b, k, m)

            def scale_output_bias(b, k, m):
                i = b * K + k
                col = (m * K + k) % 4
                e = choice(b, k)
                reached(act, gate_copied, i + 1)
                reached(act, bias_half, i - 1)
                nc.scalar.activation(bias_part[k][:], b2_wide[:].rearrange("p e d -> p (e d)")[:, bass.ds(e * D, D)], ACT.Copy,
                                     scale=gate_col[:, col:col + 1]).then_inc(bias_scaled, 1)

            expert_steps(act, expert_step)

        @block.gpsimd
        def _(pool):
            nc.gpsimd.memset(ident[:], 0.0).then_inc(ident_ready, 1)
            nc.gpsimd.memset(neg_half[:], -0.5)
            nc.gpsimd.memset(half_col[:], 0.5)
            nc.gpsimd.memset(mean_w[:], 1.0 / N)
            for e in range(E):
                nc.gpsimd.memset(e_wide[:, e:e + 1], float(e))
                nc.gpsimd.memset(e_less[:, e:e + 1], float(e - E))
            for p in range(2):
                nc.gpsimd.memset(v_hi[p][:, :, :, HEAD:VW], 1.0)
                nc.gpsimd.memset(v_mid[p][:, :, :, HEAD:VW], 0.0)
                last = nc.gpsimd.memset(v_lo[p][:, :, :, HEAD:VW], 0.0)
            last.then_inc(const_ready, 1)
            pool.wait_ge(ident_ready, 1)
            nc.gpsimd.affine_select(out=ident[:], in_=ident[:], compare_op=ALU.not_equal, fill=1.0, base=0,
                                    pattern=[[-1, P]], channel_multiplier=1).then_inc(ident_ready, 1)
            pool.wait_ge(const_ready, 1)
            pool.wait_ge(small_loaded, 16 * (3 + DC))

            def inverse_root(out_, var, exponent, eps_done, count, done):
                nc.gpsimd.tensor_scalar(out_, var, EPS, None, ALU.add).then_inc(eps_done, 1)
                reached(pool, eps_done, count)
                nc.gpsimd.tensor_tensor(out_, out_, exponent, ALU.pow).then_inc(done, 1)

            def guard(t, g):
                n = 2 * t + g
                levels = N.bit_length() - 1
                reached(pool, max_ready, 4 * (n + 1))
                width = N // 2
                nc.gpsimd.tensor_tensor(fold[:], att[g][:, :, 0:width], att[g][:, :, width:N], ALU.add).then_inc(fold_done, 1)
                for level in range(1, levels):
                    reached(pool, fold_done, levels * n + level)
                    width //= 2
                    nc.gpsimd.tensor_tensor(fold[:, :, 0:width], fold[:, :, 0:width], fold[:, :, width:2 * width],
                                            ALU.add).then_inc(fold_done, 1)
                nc.gpsimd.tensor_scalar(zero_max[:], row_max[g][:], 0.0, None, ALU.is_equal).then_inc(zero_done, 1)
                reached_before(pool, fold_done, levels * (n + 1))
                nc.gpsimd.tensor_scalar(zero_sum[:], fold[:, :, 0], 0.0, None, ALU.is_equal).then_inc(zero_done, 1)
                reached(pool, zero_done, 4 * n + 2)
                nc.gpsimd.tensor_tensor(zero_sum[:], zero_sum[:], zero_max[:], ALU.mult).then_inc(zero_done, 1)
                reached_before(pool, zero_done, 4 * n + 3)
                nc.gpsimd.tensor_scalar(keep[g][:], zero_sum[:], -1.0, 1.0, ALU.mult, ALU.add).then_inc(zero_done, 1)
                reached_before(pool, zero_done, 4 * n + 4)
                nc.gpsimd.tensor_copy(keep[g][:, 0:1], keep[g][:, 0:1]).then_inc(keep_ready, 1)

            def step(t, p, lap):
                if has(t, 0):
                    for g in range(2):
                        reached(pool, v_hi_done, 2 * t + g + 1)
                        nc.gpsimd.tensor_tensor(heads(v_sum[g]), heads(v_sum[g]), v_hi[p][:, g, :, 0:HEAD], ALU.subtract).then_inc(v_rest_done, 1)
                    for g in range(2):
                        reached(pool, v_mid_done, 2 * t + g + 1)
                        nc.gpsimd.tensor_tensor(v_lo[p][:, g, :, 0:HEAD], heads(v_sum[g]), v_mid[p][:, g, :, 0:HEAD], ALU.subtract).then_inc(v_split, 1)
                if has(t, -1):
                    reached_before(pool, mv2_ready, 2 * t)
                    inverse_root(rs2[:, 1:2], mv2[:, 1, 1:2], neg_half[:, 0:1], rs2_eps, 2 * t, rs2_ready)
                if has(t, 2):
                    reached_before(pool, mv1_ready, t + 3)
                    inverse_root(rs1[:], mv1[:, :, 1], neg_half[:], rs1_eps, t + 3, rs1_ready)
                if has(t, 0):
                    guard(t, 0)
                if has(t, 1):
                    reached(pool, x_loaded[1 - p], 16 * (lap + 1 + p))
                    if has(t, -1):
                        reached(pool, u_ready, 2 * t)
                        reached(pool, x1_stored[1 - p], 16 * (lap + p))
                    for g in range(2):
                        last = nc.gpsimd.tensor_tensor(x1_sb[1 - p][:, g, :], x_in[1 - p][:, g, :], bo_wide[:], ALU.add)
                    last.then_inc(xbo_ready, 1)
                if has(t, 0):
                    guard(t, 1)
                    reached_before(pool, mv2_ready, 2 * t + 1)
                    inverse_root(rs2[:, 0:1], mv2[:, 0, 1:2], neg_half[:, 0:1], rs2_eps, 2 * t + 1, rs2_ready)

            attention_steps(pool, step)
            pool.wait_ge(routed, 1)
            pool.wait_ge(wide_loaded, 64)

            def expert_step(b, m, lap):
                if graph(b, 1):
                    reached_before(pool, mv_u_ready, b + 2)
                    inverse_root(rs_u[:], mv_u[:, 1:2], neg_half[:, 0:1], rs_u_eps, b + 2, rs_u_ready)
                if graph(b, -2):
                    d = (m - 2) % 4
                    reached_before(pool, mv_z_ready, b - 1)
                    inverse_root(rs_z[:], mv_z[:, 1:2], neg_half[:, 0:1], rs_z_eps, b - 1, rs_z_ready)
                    reached(pool, zn_done, b - 1)
                    nc.gpsimd.tensor_tensor(z_sb[d][:], z_sb[d][:], lng_wide[:], ALU.mult).then_inc(zg_done, 1)
                    reached(pool, zg_done, b - 1)
                    nc.gpsimd.tensor_tensor(z_sb[d][:], z_sb[d][:], x1_in[d][:], ALU.add).then_inc(zx_done, 1)
                    reached(pool, zx_done, b - 1)
                    reached(pool, out_stored[m % 2], 16 * (2 * lap + m // 2 - 1))
                    nc.gpsimd.tensor_tensor(out_sb[m % 2][:], z_sb[d][:], lnb_wide[:], ALU.add).then_inc(out_ready, 1)

                if graph(b, 0):
                    for k in range(K):
                        i = b * K + k
                        reached(pool, bias_half, i)
                        reached(pool, bias_scaled, i + 1)
                        reached(pool, ut_mm, b + 1)
                        nc.gpsimd.tensor_tensor(z_sb[m][:], z_sb[m][:], bias_part[k][:], ALU.add).then_inc(bias_half, 1)

            expert_steps(pool, expert_step)

        @block.vector
        def _(dve):
            dve.wait_ge(small_loaded, 16 * (3 + DC))
            dve.wait_ge(const_ready, 1)
            for n in range(4 * DC):
                dve.wait_ge(wt_hi_done, n + 1)
                nc.vector.tensor_tensor(wt_lo[n // DC][:, n % DC, :], slot[n % 4][:, 0:D],
                                        wt_hi[n // DC][:, n % DC, :].bitcast(F32), ALU.subtract).then_inc(wt_lo_done, 1)
            nc.vector.tensor_copy(rw_wide[:].rearrange("p c e n -> p (c e) n"),
                                  rw_t[:].rearrange("p c (e o) -> p (c e) o", o=1).to_broadcast([P, DC * E, P])).then_inc(const_ready, 1)

            def add_bias_and_max(t, p, g, lap):
                n = 2 * t + g
                reached(dve, adj_loaded[p], 16 * (lap + 1))
                for r in range(QUAD):
                    reached_before(dve, s_mm, 4 * n + r + 1)
                    for c in range(DC):
                        hh = r * DC + c
                        last = nc.vector.tensor_tensor_reduce(out=att[g][:, hh, :], in0=score[r][:, c * N:(c + 1) * N], in1=adj_in[p][:, g, :],
                                                              scale=1.0, scalar=LOWEST, op0=ALU.add, op1=ALU.max,
                                                              accum_out=row_max[g][:, hh:hh + 1])
                    last.then_inc(max_ready, 1)
                    reached(dve, max_ready, 4 * n + r + 1)
                    nc.vector.tensor_scalar(neg_max[g][:, r * DC:(r + 1) * DC], row_max[g][:, r * DC:(r + 1) * DC],
                                            -1.0, None, ALU.mult).then_inc(neg_ready, 1)

            def residual(t, g, p, bank):
                n = 2 * t + g
                reached(dve, wo_mm, n + 1)
                reached(dve, xbo_ready, t + 1)
                nc.vector.tensor_tensor(x1_sb[p][:, g, :], bank[:, 0:D], x1_sb[p][:, g, :], ALU.add).then_inc(x1_done, 1)
                reached(dve, x1_done, n + 1)
                nc.vector.bn_stats(st2[:, g, :], x1_sb[p][:, g, :]).then_inc(st2_done, 1)
                reached_before(dve, st2_done, n + 1)
                nc.vector.bn_aggr(mv2[:, g, :], st2[:, g, :]).then_inc(mv2_ready, 1)

            def normalise_x1(t, g, p):
                reached(dve, rs2_ready, 2 * t + g + 1)
                nc.vector.tensor_scalar(u_att[:, g, :], x1_sb[p][:, g, :], mv2[:, g, 0:1], rs2[:, g:g + 1],
                                        ALU.subtract, ALU.mult).then_inc(u_ready, 1)

            def split_prob_lo(t, g, c, bank):
                reached(dve, pt_hi_done, PTC * (2 * t + g) + c + 1)
                nc.vector.tensor_tensor(pt_lo[c][:], bank[:], pt_hi[c][:], ALU.subtract).then_inc(pt_done, 1)

            def take_v(t, g, bank):
                reached(dve, v_mm, 2 * t + g + 1)
                reached(dve, v_split, 2 * t + g - 1)
                nc.vector.tensor_tensor(v_sum[g][:], bank[:, 0:D], bv_wide[:], ALU.add).then_inc(v_done, 1)

            def divide(t, g, bank):
                n = 2 * t + g
                reached(dve, o_mm, n + 1)
                o_ps = bank[:, 0:HEADS * VW].rearrange("p (h d) -> p h d", d=VW)
                nc.vector.reciprocal(inv_sum[g][:], o_ps[:, :, HEAD]).then_inc(inv_done, 1)
                reached(dve, inv_done, n + 1)
                reached(dve, keep_ready, n + 1)
                nc.vector.tensor_tensor(inv_kept[g][:], inv_sum[g][:], keep[g][:], ALU.mult).then_inc(kept_done, 1)
                reached(dve, kept_done, n + 1)
                nc.vector.tensor_tensor(o_sb[g][:].rearrange("p (c r d) -> p r c d", c=DC, r=QUAD),
                                        o_ps[:, :, 0:HEAD].rearrange("p (r c) d -> p r c d", r=QUAD),
                                        inv_kept[g][:].rearrange("p (r c o) -> p r c o", r=QUAD, o=1).to_broadcast([P, QUAD, DC, HEAD]),
                                        ALU.mult).then_inc(o_done, 1)

            def split_o_lo(t, g, bank):
                reached(dve, ot_hi_done, 2 * t + g + 1)
                nc.vector.tensor_tensor(ot_lo[g][:].rearrange("p c n -> p (c n)"), bank[:, 0:D],
                                        ot_hi[g][:].rearrange("p c n -> p (c n)").bitcast(F32), ALU.subtract).then_inc(ot_lo_done, 1)

            def step(t, p, lap):
                now, nxt, prev, far = has(t, 0), has(t, 1), has(t, -1), has(t, 2)
                if nxt:
                    reached(dve, xt_hi_done, 2 * (t + 1) + 1)
                    nc.vector.tensor_tensor(xt_lo[:, 0:2, :], slot[0][:].rearrange("p (c n) -> p c n", c=2),
                                            xt_hi[:, 0:2, :].bitcast(F32), ALU.subtract).then_inc(xt_lo_done, 1)
                    reached(dve, xt_hi_done, 2 * (t + 1) + 2)
                    nc.vector.tensor_tensor(xt_lo[:, 2, :], slot[1][:, 0:2 * N], xt_hi[:, 2, :].bitcast(F32),
                                            ALU.subtract).then_inc(xt_lo_done, 1)
                if now:
                    add_bias_and_max(t, p, 0, lap)
                if prev:
                    residual(t - 1, 1, 1 - p, slot[2])
                if far:
                    reached(dve, x_loaded[p], 16 * (lap + 2))
                    for g in range(2):
                        last = nc.vector.bn_stats(st1[:, g, :], x_in[p][:, g, :])
                    last.then_inc(st1_done, 1)
                    reached_before(dve, st1_done, t + 3)
                    for g in range(2):
                        last = nc.vector.bn_aggr(mv1[:, g, :], st1[:, g, :])
                    last.then_inc(mv1_ready, 1)
                if now:
                    add_bias_and_max(t, p, 1, lap)
                if nxt:
                    reached(dve, k_mm, 2 * (t + 1) + 1)
                    nc.vector.tensor_copy(k_t[1 - p][:, 0:2, :], slot[1][:].rearrange("p (c n) -> p c n", c=2)).then_inc(k_done, 1)
                    reached(dve, k_mm, 2 * (t + 1) + 2)
                    nc.vector.tensor_copy(k_t[1 - p][:, 2, :], slot[2][:, 0:2 * N]).then_inc(k_done, 1)
                if prev:
                    normalise_x1(t - 1, 1, 1 - p)
                if now:
                    for c in range(PTC):
                        split_prob_lo(t, 0, c, slot[(3, 0, 1)[c]])
                if prev:
                    reached(dve, pooled_mm, t)
                if nxt:
                    take_v(t + 1, 0, slot[2])
                if prev:
                    where = slice(2 * (t - 1), 2 * t) if isinstance(t, int) else bass.ds(t * 2 - 2, 2)
                    nc.vector.tensor_copy(pooled[:, where, :], slot[2][:, D:D + 2 * DC].rearrange("p (g c) -> p g c", g=2)).then_inc(pooled_done, 1)
                if now:
                    divide(t, 0, slot[3])
                if far:
                    reached(dve, rs1_ready, t + 3)
                    for g in range(2):
                        last = nc.vector.tensor_scalar(xn[:, g, :], x_in[p][:, g, :], mv1[:, g, 0:1], rs1[:, g:g + 1],
                                                       ALU.subtract, ALU.mult)
                    last.then_inc(xn_ready, 1)
                if now:
                    for c in range(PTC):
                        split_prob_lo(t, 1, c, slot[c])
                if nxt:
                    take_v(t + 1, 1, slot[3])
                if now:
                    split_o_lo(t, 0, slot[0])
                    divide(t, 1, slot[1])
                    residual(t, 0, p, slot[2])
                    split_o_lo(t, 1, slot[3])
                    normalise_x1(t, 0, p)

            attention_steps(dve, step)

            steps = [0]

            def chained(instruction):
                steps[0] += 1
                instruction.then_inc(route_step, 1)
                dve.wait_ge(route_step, steps[0])

            def over_experts(v):
                return v.rearrange("p (b o) -> p b o", o=1).to_broadcast([P, B, E])

            def over_graphs(v):
                return v.rearrange("p (o e) -> p o e", o=1).to_broadcast([P, B, E])

            dve.wait_ge(logit_mm, 1)
            chained(nc.vector.tensor_tensor(logit[:], slot[0][:, 0:E * B].rearrange("p (e b) -> p b e", e=E), over_graphs(rb_wide[:]), ALU.add))
            for k in range(K):
                chained(nc.vector.tensor_reduce(top[:, k, :], logit[:], AX.X, ALU.max))
                chained(nc.vector.tensor_tensor(hit[:], logit[:], over_experts(top[:, k, :]), ALU.is_equal))
                chained(nc.vector.tensor_tensor(hit[:], hit[:], over_graphs(e_less[:]), ALU.mult))
                chained(nc.vector.tensor_reduce(top_e[:, k, :], hit[:], AX.X, ALU.min))
                chained(nc.vector.tensor_scalar(top_e[:, k, :], top_e[:, k, :], float(E), None, ALU.add))
                chained(nc.vector.tensor_copy(expert[:, :, k], top_e[:, k, :]))
                if k == 0:
                    chained(nc.vector.tensor_tensor(hit[:], over_graphs(e_wide[:]), over_experts(top_e[:, k, :]), ALU.is_equal))
                    chained(nc.vector.scalar_tensor_tensor(out=logit[:], in0=hit[:], scalar=LOWEST, in1=logit[:], op0=ALU.mult, op1=ALU.add))
            nc.vector.tensor_tensor(g_tmp[:, 0, :], top[:, 1, :], top[:, 0, :], ALU.subtract).then_inc(route_exp, 1)
            dve.wait_ge(route_exp, 2)
            chained(nc.vector.tensor_scalar(g_tmp[:, 2, :], g_tmp[:, 1, :], 1.0, None, ALU.add))
            chained(nc.vector.reciprocal(g_tmp[:, 0, :], g_tmp[:, 2, :]))
            chained(nc.vector.tensor_copy(gate[:, :, 0], g_tmp[:, 0, :]))
            nc.vector.tensor_tensor(gate[:, :, 1], g_tmp[:, 0, :], g_tmp[:, 1, :], ALU.mult).then_inc(routed, 1)
            dve.wait_ge(routed, 1)

            hid_ps, at_ps, y_ps, ut_ps = score[0:2], score[2:4], slot[0:2], slot[2]

            def choice(b, k):
                i = b * K + k
                cell = expert[0:1].rearrange("p b k -> p (b k)")
                cell = cell[:, i:i + 1] if isinstance(i, int) else cell[:, bass.ds(i, 1)]
                return dve.value_load(cell, min_val=0, max_val=E - 1)

            def stats_u(b, m, lap):
                reached(dve, x1_loaded[m], 16 * (lap + 1))
                nc.vector.bn_stats(st_u[:], x1_in[m][:]).then_inc(st_u_done, 1)
                reached_before(dve, st_u_done, b + 1)
                nc.vector.bn_aggr(mv_u[:], st_u[:]).then_inc(mv_u_ready, 1)

            def normalise_u(b, m):
                reached(dve, rs_u_ready, b + 1)
                reached(dve, out_ready, b - 3)
                nc.vector.tensor_scalar(z_sb[m][:], x1_in[m][:], mv_u[:, 0:1], rs_u[:], ALU.subtract, ALU.mult).then_inc(un_ready, 1)

            def split_u_lo(b):
                reached(dve, ut_hi_done, b + 1)
                nc.vector.tensor_tensor(ut_lo[:].rearrange("p c n -> p (c n)"), ut_ps[:, 0:D],
                                        ut_hi[:].rearrange("p c n -> p (c n)").bitcast(F32), ALU.subtract).then_inc(ut_lo_done, 1)

            def split_act_lo(b, k, m):
                i = b * K + k
                col = (m * K + k) % 4
                reached(dve, at_hi_done, i + 1)
                for s in range(2):
                    last = nc.vector.scalar_tensor_tensor(out=at_lo[:, s * DC:(s + 1) * DC, :].rearrange("p c n -> p (c n)"), in0=at_ps[s][:, 0:HALF],
                                                          scalar=gate_col[:, col:col + 1],
                                                          in1=at_hi[:, s * DC:(s + 1) * DC, :].rearrange("p c n -> p (c n)").bitcast(F32),
                                                          op0=ALU.mult, op1=ALU.subtract)
                last.then_inc(at_lo_done, 1)

            def take_hidden(b, k, m):
                i = b * K + k
                col = (m * K + k) % 4
                e = choice(b, k)
                g = gate[:].rearrange("p b k -> p (b k)")
                g = g[:, i:i + 1] if isinstance(i, int) else g[:, bass.ds(i, 1)]
                nc.vector.tensor_copy(gate_col[:, col:col + 1], g).then_inc(gate_copied, 1)
                reached(dve, h_mm, i + 1)
                for s in range(2):
                    last = nc.vector.tensor_tensor(hid[k][:, s], hid_ps[s][:, 0:HALF],
                                                   b1_wide[:].rearrange("p e s f -> p (e s f)")[:, bass.ds(e * F + s * HALF, HALF)], ALU.add)
                last.then_inc(hid_done, 1)

            def activate_first(b, k):
                i = b * K + k
                e = choice(b, k)
                with dve.If(e == 1):
                    dve.wait_ge(act_done, 2 * i + 2)
                    nc.vector.tensor_tensor(hid[k][:], hid[k][:], half_t[:], ALU.mult).then_inc(a_ready[k], 1)
                with dve.Else():
                    with dve.If(e == 2):
                        dve.wait_ge(act_done, 2 * i + 1)
                        nc.vector.reciprocal(denom[:, 0], denom[:, 0]).then_inc(mish_step, 1)
                    with dve.Else():
                        dve.nop()

            def activate_second(b, k):
                i = b * K + k
                e = choice(b, k)
                with dve.If(e == 2):
                    dve.wait_ge(act_done, 2 * i + 2)
                    nc.vector.reciprocal(denom[:, 1], denom[:, 1]).then_inc(mish_step, 1)
                    nc.vector.scalar_tensor_tensor(out=hid[k][:], in0=half_t[:], scalar=1.0, in1=hid[k][:],
                                                   op0=ALU.subtract, op1=ALU.mult).then_inc(mish_step, 1)
                    dve.wait_ge(mish_step, 3 * i + 3)
                    nc.vector.scalar_tensor_tensor(out=hid[k][:], in0=denom[:], scalar=-1.0, in1=hid[k][:],
                                                   op0=ALU.mult, op1=ALU.mult).then_inc(a_ready[k], 1)
                with dve.Else():
                    dve.sem_inc(mish_step, 3)

            def add_experts(b, m):
                reached(dve, y_mm, K * (b + 1))
                reached(dve, bias_half, K * (b + 1))
                nc.vector.tensor_tensor(z_sb[m][:], y_ps[m % 2][:, 0:D], z_sb[m][:], ALU.add).then_inc(z_added, 1)
                reached(dve, z_added, b + 1)
                nc.vector.bn_stats(st_z[:], z_sb[m][:]).then_inc(st_z_done, 1)
                reached_before(dve, st_z_done, b + 1)
                nc.vector.bn_aggr(mv_z[:], st_z[:]).then_inc(mv_z_ready, 1)

            def normalise_z(b, m):
                reached(dve, rs_z_ready, b + 1)
                nc.vector.tensor_scalar(z_sb[m][:], z_sb[m][:], mv_z[:, 0:1], rs_z[:], ALU.subtract, ALU.mult).then_inc(zn_done, 1)

            def split_weights(first, end):
                for m in range(first, end):
                    hi = w1_hi[:, m].rearrange("p c f -> p (c f)") if m < E else w2_hi[:, m - E].rearrange("p c d -> p (c d)")
                    lo = w1_lo[:, m].rearrange("p c f -> p (c f)") if m < E else w2_lo[:, m - E].rearrange("p c d -> p (c d)")
                    dve.wait_ge(split_hi, m + 1)
                    nc.vector.tensor_tensor(lo, w_stage[m % 2][:], hi.bitcast(F32), ALU.subtract).then_inc(split_lo, 1)

            def expert_step(b, m, lap):
                first = isinstance(b, int) and b == -1
                for k in range(K):
                    if graph(b, -1):
                        split_act_lo(b - 1, k, m - 1)
                    if graph(b - (1 - k), 0):
                        activate_second(b - (1 - k), 1 - k)
                    if graph(b, 0):
                        if isinstance(b, int) and b == 0 and k == 0:
                            dve.wait_ge(split_lo, 2 * E)
                            dve.wait_ge(wide_loaded, 64)
                        take_hidden(b, k, m)
                    if k == 0 and graph(b, 1):
                        stats_u(b + 1, (m + 1) % 4, lap + (m + 1) // 4)
                    if k == 0 and graph(b, -2):
                        add_experts(b - 2, (m - 2) % 4)
                    if k == 1 and graph(b, 1):
                        if first:
                            split_weights(0, 2)
                        split_u_lo(b + 1)
                        if first:
                            split_weights(2, 2 * E)
                    if graph(b, 0):
                        activate_first(b, k)
                    if k == 0 and graph(b, 1):
                        normalise_u(b + 1, (m + 1) % 4)
                    if k == 0 and graph(b, -2):
                        normalise_z(b - 2, (m - 2) % 4)

            expert_steps(dve, expert_step)


_INS = ["x", "adj", "L0_gnn_Wq", "L0_gnn_Wk", "L0_gnn_Wv", "L0_gnn_bv", "L0_gnn_Wo", "L0_gnn_bo", "L0_ffn_router_w",
        "L0_ffn_router_b", "L0_ffn_w1", "L0_ffn_b1", "L0_ffn_w2", "L0_ffn_b2", "L0_ffn_ln_g", "L0_ffn_ln_b"]


def kernel(**inputs):
    import numpy as np
    import concourse.bacc as bacc
    from concourse.bass_utils import run_bass_kernel_spmd

    nc = bacc.Bacc("TRN2", target_bir_lowering=False, num_devices=1)
    arrays, args = {}, []
    for name in _INS:
        a = np.ascontiguousarray(inputs[name])
        arrays[f"in_{name}"] = a
        args.append(nc.dram_tensor(f"in_{name}", a.shape, mybir.dt.from_np(a.dtype), kind="ExternalInput").ap())
    out = nc.dram_tensor("out_dram", inputs["x"].shape, F32, kind="ExternalOutput").ap()
    gnn_moe_kernel(nc, *args, out)
    r = run_bass_kernel_spmd(nc, [arrays], core_ids=[0])
    return r.results[0]["out_dram"]
```

```python
from contextlib import ExitStack

import concourse.bass as bass
from concourse import mybir

F32 = mybir.dt.float32
F32R = mybir.dt.float32r
I32 = mybir.dt.int32
F16 = mybir.dt.float16
BF16 = mybir.dt.bfloat16
ALU = mybir.AluOpType
ACT = mybir.ActivationFunctionType
AX = mybir.AxisListType

P = 128
BANK = 512
EPS = 1e-5
LOWEST = -3.4028234e38
SEED_G, SEED_B, SEED_D = 0.14768684, -1.47317444, 0.67629098
SILU, MISH = 1, 2


def reached(engine, semaphore, count):
    if not isinstance(count, int) or count > 0:
        engine.wait_ge(semaphore, count)


def gnn_moe_kernel(nc, x, adj, Wq, Wk, Wv, bv, Wo, bo, router_w, router_b, w1, b1, w2, b2, ln_g, ln_b, out):
    B, N, D = x.shape
    E, _, F = w1.shape
    HEAD = 32
    HEADS = D // HEAD
    DC = D // P
    FC = F // P
    QUAD = P // HEAD
    PAIRS = B // 2
    K = 2
    SCALE = float(D) ** -0.5
    VW = HEAD + 1
    PTC = HEADS * N // BANK
    HPB = BANK // N
    HALF = F // 2
    assert N == P and D % P == 0 and F % P == 0 and HALF <= BANK and B % 4 == 0 and QUAD * DC == HEADS

    x1_dram = nc.dram_tensor("x1_scratch", (B, N, D), F32, kind="Internal").ap()

    with ExitStack() as ctx:
        def sb(name, shape, dt=F32, to=ctx):
            return to.enter_context(nc.sbuf_tensor(name, shape, dt))

        def ps(name, shape, dt=F32):
            return ctx.enter_context(nc.psum_tensor(name, shape, dt))

        def sem(name):
            return ctx.enter_context(nc.semaphore(name))

        ident = sb("ident", [P, P])
        mean_w = sb("mean_w", [P, 1])
        one_col = sb("one_col", [P, 1])
        half_col = sb("half_col", [P, 1])
        seed_in = sb("seed_in", [P, 1])
        seed_out = sb("seed_out", [P, 1])
        neg_half = sb("neg_half", [P, 2])
        pooled = sb("pooled", [P, B, DC])
        gate = sb("gate", [P, B, K, 2])
        expert = sb("expert", [P, B, K], I32)

        st_u = sb("st_u", [P, 6])
        mv_u = sb("mv_u", [P, 2])
        rs_u = sb("rs_u", [P, 1])
        st_z = sb("st_z", [P, 6])
        mv_z = sb("mv_z", [P, 2])
        rs_z = sb("rs_z", [P, 1])
        gate_col = sb("gate_col", [P, 4, 2])
        w1_lo = sb("w1_lo", [P, E, DC, F], F32R)

        s1 = ExitStack()
        wt_hi = [sb(f"wt_hi{m}", [P, DC, D], F32R, s1) for m in range(4)]
        wt_lo = [sb(f"wt_lo{m}", [P, DC, D], F32R, s1) for m in range(4)]
        w_raw = [sb(f"w_raw{m}", [P, DC, D], F32, s1) for m in range(4)]
        xt_hi = sb("xt_hi", [P, DC, 2 * N], F32R, s1)
        xt_lo = sb("xt_lo", [P, DC, 2 * N], F32R, s1)
        q_t = [sb(f"q_t{p}", [P, DC, 2 * N], F32, s1) for p in range(2)]
        k_t = [sb(f"k_t{p}", [P, DC, 2 * N], F32, s1) for p in range(2)]
        v_sum = [sb(f"v_sum{g}", [P, D], F32, s1) for g in range(2)]
        v_hi = [sb(f"v_hi{p}", [P, 2, HEADS, VW], BF16, s1) for p in range(2)]
        v_mid = [sb(f"v_mid{p}", [P, 2, HEADS, VW], BF16, s1) for p in range(2)]
        v_lo = [sb(f"v_lo{p}", [P, 2, HEADS, VW], BF16, s1) for p in range(2)]
        att = [sb(f"att{g}", [P, HEADS, N], F32, s1) for g in range(2)]
        prob = [sb(f"prob{g}", [P, HEADS, N], F32, s1) for g in range(2)]
        pt_hi = [sb(f"pt_hi{c}", [P, BANK], F16, s1) for c in range(PTC)]
        pt_lo = [sb(f"pt_lo{c}", [P, BANK], F16, s1) for c in range(PTC)]
        o_sb = [sb(f"o_sb{g}", [P, D], F32, s1) for g in range(2)]
        ot_hi = [sb(f"ot_hi{g}", [P, DC, N], F32R, s1) for g in range(2)]
        ot_lo = [sb(f"ot_lo{g}", [P, DC, N], F32R, s1) for g in range(2)]
        fold = sb("fold", [P, HEADS, N // 2], F32, s1)
        adj_in = [sb(f"adj_in{p}", [P, 2, N], F32, s1) for p in range(2)]
        xn = sb("xn", [P, 2, D], F32, s1)
        x_in = [sb(f"x_in{p}", [P, 2, D], F32, s1) for p in range(2)]
        x1_sb = [sb(f"x1_sb{p}", [P, 2, D], F32, s1) for p in range(2)]
        u_att = sb("u_att", [P, 2, D], F32, s1)
        rw_t = sb("rw_t", [P, DC, E], F32, s1)
        rw_wide = sb("rw_wide", [P, DC, E, P], F32, s1)
        rb_wide = sb("rb_wide", [P, E], F32, s1)
        bv_wide = sb("bv_wide", [P, D], F32, s1)
        bo_wide = sb("bo_wide", [P, D], F32, s1)
        row_max = [sb(f"row_max{g}", [P, HEADS], F32, s1) for g in range(2)]
        neg_max = [sb(f"neg_max{g}", [P, HEADS], F32, s1) for g in range(2)]
        keep = [sb(f"keep{g}", [P, HEADS], F32, s1) for g in range(2)]
        zero_max = sb("zero_max", [P, HEADS], F32, s1)
        zero_sum = sb("zero_sum", [P, HEADS], F32, s1)
        inv_sum = [sb(f"inv_sum{g}", [P, HEADS], F32, s1) for g in range(2)]
        inv_kept = [sb(f"inv_kept{g}", [P, HEADS], F32, s1) for g in range(2)]
        st1 = sb("st1", [P, 2, 6], F32, s1)
        mv1 = sb("mv1", [P, 2, 2], F32, s1)
        rs1 = sb("rs1", [P, 2], F32, s1)
        st2 = sb("st2", [P, 2, 6], F32, s1)
        mv2 = sb("mv2", [P, 2, 2], F32, s1)
        rs2 = sb("rs2", [P, 2], F32, s1)
        e_wide = sb("e_wide", [P, E], F32, s1)
        e_less = sb("e_less", [P, E], F32, s1)
        logit = sb("logit", [P, B, E], F32, s1)
        hit = sb("hit", [P, B, E], F32, s1)
        top = sb("top", [P, K, B], F32, s1)
        top_e = sb("top_e", [P, K, B], F32, s1)
        g_tmp = sb("g_tmp", [P, 3, B], F32, s1)
        factor = sb("factor", [P, 2, K, B], F32, s1)
        s1.close()

        w1_hi = sb("w1_hi", [P, E, DC, F], F32R)
        w2_lo = sb("w2_lo", [P, E, FC, D], F32R)
        w2_hi = sb("w2_hi", [P, E, FC, D], F32R)
        x1_in = [sb(f"x1_in{m}", [P, D]) for m in range(4)]
        z_sb = [sb(f"z_sb{m}", [P, D]) for m in range(4)]
        ut_hi = sb("ut_hi", [P, DC, N], F32R)
        ut_lo = sb("ut_lo", [P, DC, N], F32R)
        b1_wide = sb("b1_wide", [P, E, 2, HALF])
        b2_wide = sb("b2_wide", [P, E, D])
        lng_wide = sb("lng_wide", [P, D])
        lnb_wide = sb("lnb_wide", [P, D])
        bias_part = [sb(f"bias_part{k}", [P, D]) for k in range(K)]
        hid = [sb(f"hid{k}", [P, 2, HALF]) for k in range(K)]
        half_t = sb("half_t", [P, 2, HALF])
        inverse = sb("inverse", [P, 2, HALF])
        miss2 = sb("miss2", [P, 2, HALF])
        at_hi = sb("at_hi", [P, FC, N], F32R)
        at_lo = sb("at_lo", [P, FC, N], F32R)

        score = [ps(f"score{r}", [P, BANK]) for r in range(4)]
        slot = [ps(f"slot{r}", [P, BANK]) for r in range(4)]

        passed = sem("passed")

        def reached_before(engine, semaphore, count):
            reached(engine, semaphore, count)
            if not isinstance(count, int):
                engine.sem_inc(passed, 1)

        const_ready = sem("const_ready")
        small_loaded = sem("small_loaded")
        w_loaded = [sem(f"w_loaded{m}") for m in range(4)]
        ident_ready = sem("ident_ready")
        wt_mm, wt_hi_done, wt_lo_done = sem("wt_mm"), sem("wt_hi_done"), sem("wt_lo_done")
        x_loaded = [sem(f"x_loaded{p}") for p in range(2)]
        adj_loaded = [sem(f"adj_loaded{p}") for p in range(2)]
        x1_stored = [sem(f"x1_stored{p}") for p in range(2)]
        st1_done, mv1_ready, rs1_eps, rs1_ready = sem("st1_done"), sem("mv1_ready"), sem("rs1_eps"), sem("rs1_ready")
        xn_ready = sem("xn_ready")
        xt_mm, xt_hi_done, xt_lo_done = sem("xt_mm"), sem("xt_hi_done"), sem("xt_lo_done")
        q_mm, q_done = sem("q_mm"), sem("q_done")
        k_mm, k_done = sem("k_mm"), sem("k_done")
        v_mm, v_done = sem("v_mm"), sem("v_done")
        v_hi_done, v_rest_done, v_mid_done, v_split = sem("v_hi_done"), sem("v_rest_done"), sem("v_mid_done"), sem("v_split")
        s_mm, max_ready, neg_ready = sem("s_mm"), sem("max_ready"), sem("neg_ready")
        exp_done = sem("exp_done")
        fold_done, zero_done, keep_ready = sem("fold_done"), sem("zero_done"), sem("keep_ready")
        pt_mm, pt_hi_done, pt_done = sem("pt_mm"), sem("pt_hi_done"), sem("pt_done")
        o_mm, inv_done, kept_done, o_done = sem("o_mm"), sem("inv_done"), sem("kept_done"), sem("o_done")
        ot_mm, ot_hi_done, ot_lo_done = sem("ot_mm"), sem("ot_hi_done"), sem("ot_lo_done")
        wo_mm, xbo_ready, x1_done = sem("wo_mm"), sem("xbo_ready"), sem("x1_done")
        st2_done, mv2_ready, rs2_eps, rs2_ready = sem("st2_done"), sem("mv2_ready"), sem("rs2_eps"), sem("rs2_ready")
        u_ready, pooled_mm, pooled_done = sem("u_ready"), sem("pooled_mm"), sem("pooled_done")
        logit_mm, route_step, route_exp, routed = sem("logit_mm"), sem("route_step"), sem("route_exp"), sem("routed")
        w1_loaded, w2_loaded = sem("w1_loaded"), [sem(f"w2_loaded{e}") for e in range(E)]
        wide_loaded = sem("wide_loaded")
        split_hi, vector_lo, gpsimd_lo = sem("split_hi"), sem("vector_lo"), sem("gpsimd_lo")
        x1_loaded = [sem(f"x1_loaded{m}") for m in range(4)]
        out_stored = [sem(f"out_stored{m}") for m in range(4)]
        st_u_done, mv_u_ready, rs_u_eps, rs_u_ready = sem("st_u_done"), sem("mv_u_ready"), sem("rs_u_eps"), sem("rs_u_ready")
        st_z_done, mv_z_ready, rs_z_eps, rs_z_ready = sem("st_z_done"), sem("mv_z_ready"), sem("rs_z_eps"), sem("rs_z_ready")
        un_ready, ut_mm, ut_hi_done, ut_lo_done = sem("un_ready"), sem("ut_mm"), sem("ut_hi_done"), sem("ut_lo_done")
        h_mm, hid_done = sem("h_mm"), sem("hid_done")
        tanh_done, square_done, seed_half, seed_done = sem("tanh_done"), sem("square_done"), sem("seed_half"), sem("seed_done")
        miss_done, newton_done, miss2_done, inverse_done = sem("miss_done"), sem("newton_done"), sem("miss2_done"), sem("inverse_done")
        a_ready = [sem(f"a_ready{k}") for k in range(K)]
        at_mm, at_hi_done, at_lo_done = sem("at_mm"), sem("at_hi_done"), sem("at_lo_done")
        gate_copied, y_mm = sem("gate_copied"), sem("y_mm")
        bias_scaled, bias_half, z_added, zn_done = sem("bias_scaled"), sem("bias_half"), sem("z_added"), sem("zn_done")
        zg_done, zx_done, out_ready = sem("zg_done"), sem("zx_done"), sem("out_ready")

        block = ctx.enter_context(nc.Block())

        def attention_steps(engine, step):
            for t in range(-2, 2):
                step(t, t % 2, t // 2)
            with engine.Fori(1, PAIRS // 2 - 1) as i:
                for p in range(2):
                    step(i * 2 + p, p, i)
            for t in range(PAIRS - 2, PAIRS + 1):
                step(t, t % 2, t // 2)

        def has(t, ahead):
            return not isinstance(t, int) or 0 <= t + ahead < PAIRS

        def expert_steps(engine, step):
            for b in range(4):
                step(b, b % 4, b // 4)
            with engine.Fori(1, B // 4 - 1) as i:
                for m in range(4):
                    step(i * 4 + m, m, i)
            for b in range(B - 4, B + 2):
                step(b, b % 4, b // 4)

        VECTOR_SPLITS = [0, 1, 2 * E - 2, 2 * E - 1]
        GPSIMD_SPLITS = [m for m in range(2 * E) if m not in VECTOR_SPLITS]

        def expert_weights(m):
            hi, lo = (w1_hi, w1_lo) if m < E else (w2_hi, w2_lo)
            return tuple(w[:, m % E].rearrange("p c n -> p (c n)") for w in (hi, lo))

        def lo_splits(splits, end):
            return sum(m < end for m in splits)

        def heads(v):
            return v[:].rearrange("p (h d) -> p h d", h=HEADS)

        def graph(b, ahead):
            return not isinstance(b, int) or 0 <= b + ahead < B

        @block.sync
        def _(sp):
            sp.dma_start(x_in[0][:], x[0:2].rearrange("g n d -> n g d")).then_inc(x_loaded[0], 16)
            for m, w in enumerate((Wq, Wk, Wv, Wo)):
                sp.dma_start(w_raw[m][:], w.rearrange("(c p) d -> p c d", p=P)).then_inc(w_loaded[m], 16)
            sp.dma_start(x_in[1][:], x[2:4].rearrange("g n d -> n g d")).then_inc(x_loaded[1], 16)
            for m in range(2):
                sp.dma_start(adj_in[m][:], adj[2 * m:2 * m + 2].rearrange("g n d -> n g d")).then_inc(adj_loaded[m], 16)
            sp.dma_start(bv_wide[:], bv.rearrange("(o d) -> o d", o=1).partition_broadcast(P)).then_inc(small_loaded, 16)
            sp.dma_start(bo_wide[:], bo.rearrange("(o d) -> o d", o=1).partition_broadcast(P)).then_inc(small_loaded, 16)
            sp.dma_start(rb_wide[:], router_b.rearrange("(o d) -> o d", o=1).partition_broadcast(P)).then_inc(small_loaded, 16)
            for c in range(DC):
                sp.dma_start(rw_t[:, c, :], router_w[:, c * P:(c + 1) * P].rearrange("e p -> p e"), allow_slow_non_contiguous=True).then_inc(small_loaded, 16)

            for e in range(E):
                sp.dma_start(w1_lo[:, e].bitcast(F32), w1[e].rearrange("(c p) f -> p c f", p=P)).then_inc(w1_loaded, 16)

            def step(t, p, lap):
                if has(t, 0) and has(t, 2):
                    reached(sp, xbo_ready, t + 1)
                    reached(sp, xn_ready, t + 1)
                    sp.dma_start(x_in[p][:], x[pair(t, 2)].rearrange("g n d -> n g d")).then_inc(x_loaded[p], 16)
                if has(t, -1):
                    reached(sp, x1_done, 2 * t)
                    sp.dma_start(x1_dram[pair(t, -1)].rearrange("g n d -> n g d"), x1_sb[1 - p][:]).then_inc(x1_stored[1 - p], 16)
                if has(t, 0) and has(t, 2):
                    reached(sp, neg_ready, 8 * (t + 1))
                    sp.dma_start(adj_in[p][:], adj[pair(t, 2)].rearrange("g n d -> n g d")).then_inc(adj_loaded[p], 16)
                if isinstance(t, int) and t == PAIRS - 1:
                    sp.wait_ge(s_mm, QUAD * B)
                    for e in range(E):
                        sp.dma_start(w2_lo[:, e].bitcast(F32), w2[e].rearrange("(c p) d -> p c d", p=P)).then_inc(w2_loaded[e], 16)

            def pair(t, ahead):
                return slice(2 * (t + ahead), 2 * (t + ahead) + 2) if isinstance(t, int) else bass.ds(t * 2 + 2 * ahead, 2)

            attention_steps(sp, step)

            for m in range(4):
                sp.wait_ge(x1_stored[m // 2], 16)
                sp.dma_start(x1_in[m][:], x1_dram[m]).then_inc(x1_loaded[m], 16)
            sp.dma_start(b1_wide[:].rearrange("p e s f -> p (e s f)"), b1.rearrange("(o e) f -> o (e f)", o=1).partition_broadcast(P)).then_inc(wide_loaded, 16)
            for p in range(2):
                sp.wait_ge(x1_stored[p], 16 * (PAIRS // 2))
            sp.wait_ge(pooled_mm, PAIRS)
            sp.dma_start(b2_wide[:].rearrange("p e d -> p (e d)"), b2.rearrange("(o e) d -> o (e d)", o=1).partition_broadcast(P)).then_inc(wide_loaded, 16)
            sp.dma_start(lng_wide[:], ln_g.rearrange("(o d) -> o d", o=1).partition_broadcast(P)).then_inc(wide_loaded, 16)
            sp.dma_start(lnb_wide[:], ln_b.rearrange("(o d) -> o d", o=1).partition_broadcast(P)).then_inc(wide_loaded, 16)

            def finish(b, m):
                reached(sp, out_ready, b + 1)
                sp.dma_start(one(out, b, 0), z_sb[m][:]).then_inc(out_stored[m], 16)
                if graph(b, 4):
                    sp.dma_start(x1_in[m][:], one(x1_dram, b, 4)).then_inc(x1_loaded[m], 16)

            def one(tensor, b, ahead):
                return tensor[b + ahead] if isinstance(b, int) else tensor[bass.ds(b + ahead, 1)].rearrange("o n d -> (o n) d")

            with sp.Fori(0, B // 4 - 1) as i:
                for m in range(4):
                    sp.wait_ge(out_ready, i * 4 + m + 1)
                    sp.dma_start(one(out, i * 4 + m, 0), z_sb[m][:]).then_inc(out_stored[m], 16)
                    sp.dma_start(x1_in[m][:], one(x1_dram, i * 4 + m, 4)).then_inc(x1_loaded[m], 16)
            for b in range(B - 4, B):
                finish(b, b % 4)
            for m in range(4):
                sp.wait_ge(out_stored[m], 16 * (B // 4))

        @block.tensor
        def _(pe):
            def split_product(acc, lhs, rhs, start=True, stop=True):
                terms = [(a, b, c) for c in range(len(lhs)) for a, b in ((0, 0), (0, 1), (1, 0))]
                for n, (a, b, c) in enumerate(terms):
                    last = nc.tensor.matmul(acc, lhs[c][a], rhs[c][b], start=start and n == 0,
                                            stop=stop and n == len(terms) - 1)
                return last

            pe.wait_ge(ident_ready, 2)
            for m in range(4):
                pe.wait_ge(w_loaded[m], 16)
                for dc in range(DC):
                    n = m * DC + dc
                    if n >= 4:
                        pe.wait_ge(wt_lo_done, n - 3)
                    for oc in range(DC):
                        last = nc.tensor.transpose(slot[n % 4][:, oc * P:(oc + 1) * P],
                                                   w_raw[m][:, oc, dc * P:(dc + 1) * P], ident[:])
                    last.then_inc(wt_mm, 1)

            def project_t(dst, m, oc):
                return split_product(dst, [(wt_hi[m][:, c, oc * P:(oc + 1) * P], wt_lo[m][:, c, oc * P:(oc + 1) * P]) for c in range(DC)],
                                     [(xt_hi[:, c, :], xt_lo[:, c, :]) for c in range(DC)])

            def project_two(m, first, second, done):
                for oc in range(DC):
                    bank = first if oc < 2 else second
                    last = project_t(bank[:, (oc % 2) * 2 * N:(oc % 2 + 1) * 2 * N], m, oc)
                    if oc > 0:
                        last.then_inc(done, 1)

            def project_v(dst, g):
                split_product(dst[:, 0:D], [(xt_hi[:, c, g * N:(g + 1) * N], xt_lo[:, c, g * N:(g + 1) * N]) for c in range(DC)],
                              [(wt_hi[2][:, c, :], wt_lo[2][:, c, :]) for c in range(DC)]).then_inc(v_mm, 1)

            def scores(t, p, g):
                for r in range(QUAD):
                    reached(pe, neg_ready, 4 * (2 * t + g - 1) + r + 1)
                    for c in range(DC):
                        rows = slice(HEAD * r, HEAD * (r + 1))
                        last = nc.tensor.matmul(score[r][:, c * N:(c + 1) * N], q_t[p][rows, c, g * N:(g + 1) * N],
                                                k_t[p][rows, c, g * N:(g + 1) * N], start=True, stop=True)
                    last.then_inc(s_mm, 1)

            def transpose_probs(t, g, c, bank):
                reached(pe, exp_done, HEADS * (2 * t + g) + HPB * (c + 1))
                for i in range(HPB):
                    last = nc.tensor.transpose(bank[:, i * N:(i + 1) * N], prob[g][:, c * HPB + i, :], ident[:])
                last.then_inc(pt_mm, 1)

            def attend(t, p, g, bank):
                reached(pe, pt_done, PTC * (2 * t + g) + PTC)
                reached(pe, v_split, 2 * t + g + 1)
                for hh in range(HEADS):
                    h = QUAD * (hh % DC) + hh // DC
                    cols = slice((hh % HPB) * N, (hh % HPB + 1) * N)
                    hi, lo = pt_hi[hh // HPB][:, cols], pt_lo[hh // HPB][:, cols]
                    terms = [(hi, v_hi), (hi, v_mid), (hi, v_lo), (lo, v_hi), (lo, v_mid)]
                    for n, (pt, v) in enumerate(terms):
                        last = nc.tensor.matmul(bank[:, hh * VW:(hh + 1) * VW], pt, v[p][:, g, h, :],
                                                start=n == 0, stop=n == len(terms) - 1)
                last.then_inc(o_mm, 1)

            def transpose_o(t, g, bank):
                reached(pe, o_done, 2 * t + g + 1)
                for c in range(DC):
                    last = nc.tensor.transpose(bank[:, c * N:(c + 1) * N], o_sb[g][:, c * P:(c + 1) * P], ident[:])
                last.then_inc(ot_mm, 1)

            def project_o(t, g, bank):
                reached(pe, ot_lo_done, 2 * t + g + 1)
                split_product(bank[:, 0:D], [(ot_hi[g][:, c, :], ot_lo[g][:, c, :]) for c in range(DC)],
                              [(wt_hi[3][:, c, :], wt_lo[3][:, c, :]) for c in range(DC)]).then_inc(wo_mm, 1)

            def pool_nodes(t, bank):
                reached(pe, u_ready, 2 * (t + 1))
                for g in range(2):
                    for c in range(DC):
                        col = HEADS * VW + g * DC + c
                        last = nc.tensor.matmul(bank[:, col:col + 1], u_att[:, g, c * P:(c + 1) * P], mean_w[:], start=True, stop=True)
                last.then_inc(pooled_mm, 1)

            def step(t, p, lap):
                now, nxt, prev = has(t, 0), has(t, 1), has(t, -1)
                if isinstance(t, int) and t == -1:
                    pe.wait_ge(wt_lo_done, 4 * DC)
                if isinstance(t, int) and t == 0:
                    pe.wait_ge(q_done, 2)
                    pe.wait_ge(k_done, 2)
                    pe.wait_ge(v_done, 2)
                if nxt:
                    reached(pe, xn_ready, t + 2)
                    for c in range(DC):
                        for g in range(2):
                            last = nc.tensor.transpose(slot[c // 2][:, ((c % 2) * 2 + g) * N:((c % 2) * 2 + g + 1) * N],
                                                       xn[:, g, c * P:(c + 1) * P], ident[:])
                        if c > 0:
                            last.then_inc(xt_mm, 1)
                if now:
                    reached(pe, q_done, 2 * (t + 1))
                    reached(pe, k_done, 2 * (t + 1))
                    scores(t, p, 0)
                if prev:
                    reached(pe, x1_done, 2 * t - 1)
                    project_o(t - 1, 1, slot[2])
                if nxt:
                    reached(pe, xt_lo_done, 2 * (t + 2))
                    reached(pe, ot_lo_done, 2 * t)
                    project_two(0, slot[3], slot[0], q_mm)
                if now:
                    scores(t, p, 1)
                if prev:
                    reached(pe, x1_done, 2 * t)
                if nxt:
                    project_two(1, slot[1], slot[2], k_mm)
                if now:
                    if nxt:
                        reached(pe, q_done, 2 * (t + 1) + 2)
                    else:
                        reached(pe, ot_lo_done, 2 * t)
                    transpose_probs(t, 0, 0, slot[3])
                    transpose_probs(t, 0, 1, slot[0])
                    if nxt:
                        reached(pe, k_done, 2 * (t + 1) + 1)
                    else:
                        reached(pe, o_done, 2 * t)
                    transpose_probs(t, 0, 2, slot[1])
                if nxt:
                    reached(pe, k_done, 2 * (t + 1) + 2)
                if nxt:
                    project_v(slot[2], 0)
                if now:
                    attend(t, p, 0, slot[3])
                    transpose_probs(t, 1, 0, slot[0])
                    transpose_probs(t, 1, 1, slot[1])
                    if nxt:
                        reached(pe, v_done, 2 * (t + 1) + 1)
                    transpose_probs(t, 1, 2, slot[2])
                    reached(pe, o_done, 2 * t + 1)
                elif nxt:
                    reached(pe, q_done, 2 * (t + 1) + 1)
                if nxt:
                    project_v(slot[3], 1)
                if now:
                    reached(pe, pt_done, PTC * (2 * t + 1) + 1)
                    transpose_o(t, 0, slot[0])
                if prev:
                    if now:
                        reached(pe, pt_done, PTC * (2 * t + 1) + 2)
                    pool_nodes(t - 1, slot[1])
                if now:
                    attend(t, p, 1, slot[1])
                    project_o(t, 0, slot[2])
                    if nxt:
                        reached(pe, v_done, 2 * (t + 1) + 2)
                    transpose_o(t, 1, slot[3])

            attention_steps(pe, step)

            pe.wait_ge(pooled_done, PAIRS)
            for e in range(E):
                for c in range(DC):
                    last = nc.tensor.matmul(slot[0][:, e * B:(e + 1) * B], rw_wide[:, c, e, :], pooled[:, :, c],
                                            start=c == 0, stop=c == DC - 1)
            last.then_inc(logit_mm, 1)

            hid_ps, at_ps, y_ps, ut_ps = score[0:2], score[2:4], slot[0:2], slot[2]

            def transpose_u(b, m):
                reached(pe, un_ready, b + 1)
                reached(pe, ut_lo_done, b)
                for c in range(DC):
                    last = nc.tensor.transpose(ut_ps[:, c * N:(c + 1) * N], z_sb[m][:, c * P:(c + 1) * P], ident[:])
                last.then_inc(ut_mm, 1)

            transpose_u(0, 0)
            pe.wait_ge(routed, 1)

            def choice(b, k):
                i = b * K + k
                cell = expert[0:1].rearrange("p b k -> p (b k)")
                cell = cell[:, i:i + 1] if isinstance(i, int) else cell[:, bass.ds(i, 1)]
                return pe.value_load(cell, min_val=0, max_val=E - 1)

            def transpose_act(b, k):
                i = b * K + k
                reached(pe, at_lo_done, 2 * i)
                for c in range(FC):
                    if c % DC == 0:
                        reached(pe, a_ready[k], 2 * b + c // DC + 1)
                    last = nc.tensor.transpose(at_ps[c // DC][:, (c % DC) * P:(c % DC + 1) * P],
                                               hid[k][:, c // DC, (c % DC) * P:(c % DC + 1) * P], ident[:])
                last.then_inc(at_mm, 1)

            def first_layer(b, k, e):
                i = b * K + k
                reached(pe, ut_lo_done, b + 1)
                for s in range(2):
                    reached(pe, hid_done, 2 * i + s - 1)
                    last = split_product(hid_ps[s][:, 0:HALF], [(ut_hi[:, c, :], ut_lo[:, c, :]) for c in range(DC)],
                                         [tuple(w[:].rearrange("p e c f -> p (e c f)")[:, bass.ds(e * (DC * F) + (c * F + s * HALF), HALF)]
                                                for w in (w1_hi, w1_lo)) for c in range(DC)])
                last.then_inc(h_mm, 1)

            def second_layer(b, k, m, e):
                i = b * K + k
                if k == 0:
                    reached(pe, z_added, b - 1)
                for s in range(2):
                    reached(pe, at_lo_done, 2 * i + s + 1)
                    chunks = range(s * DC, (s + 1) * DC)
                    last = split_product(y_ps[m % 2][:, 0:D], [(at_hi[:, c, :], at_lo[:, c, :]) for c in chunks],
                                         [tuple(w[:].rearrange("p e c d -> p (e c d)")[:, bass.ds(e * (FC * D) + c * D, D)]
                                                for w in (w2_hi, w2_lo)) for c in chunks],
                                         start=k == 0 and s == 0, stop=k == K - 1 and s == 1)
                last.then_inc(y_mm, 1)

            def expert_step(b, m, lap):
                for k in range(K):
                    first_e = choice(b, k) if graph(b, 0) else None
                    if graph(b, -1):
                        second_e = choice(b - 1, k)
                        transpose_act(b - 1, k)
                    if graph(b, 0):
                        if isinstance(b, int) and b == 0 and k == 0:
                            pe.wait_ge(vector_lo, lo_splits(VECTOR_SPLITS, E))
                            pe.wait_ge(gpsimd_lo, lo_splits(GPSIMD_SPLITS, E))
                        first_layer(b, k, first_e)
                    if k == 1 and graph(b, 1):
                        transpose_u(b + 1, (m + 1) % 4)
                    if graph(b, -1):
                        if isinstance(b, int) and b == 1 and k == 0:
                            pe.wait_ge(vector_lo, len(VECTOR_SPLITS))
                            pe.wait_ge(gpsimd_lo, len(GPSIMD_SPLITS))
                        second_layer(b - 1, k, m - 1, second_e)

            expert_steps(pe, expert_step)

        @block.scalar
        def _(act):
            for n in range(4 * DC):
                act.wait_ge(wt_mm, n + 1)
                nc.scalar.activation(wt_hi[n // DC][:, n % DC, :], slot[n % 4][:, 0:D], ACT.Copy).then_inc(wt_hi_done, 1)

            def exps(t, g, quadrants=range(QUAD)):
                for r in quadrants:
                    reached(act, neg_ready, 4 * (2 * t + g) + r + 1)
                    for c in range(DC):
                        hh = r * DC + c
                        nc.scalar.activation(prob[g][:, hh, :], att[g][:, hh, :], ACT.Exp,
                                             bias=neg_max[g][:, hh:hh + 1]).then_inc(exp_done, 1)

            def step(t, p, lap):
                now, nxt = has(t, 0), has(t, 1)
                if nxt:
                    reached(act, xt_mm, 2 * (t + 1) + 1)
                    nc.scalar.activation(xt_hi[:, 0:2, :], slot[0][:].rearrange("p (c n) -> p c n", c=2), ACT.Copy).then_inc(xt_hi_done, 1)
                    reached(act, xt_mm, 2 * (t + 1) + 2)
                    nc.scalar.activation(xt_hi[:, 2, :], slot[1][:, 0:2 * N], ACT.Copy).then_inc(xt_hi_done, 1)
                if now:
                    for g in range(2):
                        reached(act, v_done, 2 * t + g + 1)
                        nc.scalar.activation(v_hi[p][:, g, :, 0:HEAD], heads(v_sum[g]), ACT.Copy).then_inc(v_hi_done, 1)
                    for g in range(2):
                        reached(act, v_rest_done, 2 * t + g + 1)
                        nc.scalar.activation(v_mid[p][:, g, :, 0:HEAD], heads(v_sum[g]), ACT.Copy).then_inc(v_mid_done, 1)
                    exps(t, 0)
                if nxt:
                    reached(act, q_mm, 2 * (t + 1) + 1)
                    nc.scalar.activation(q_t[1 - p][:, 0:2, :], slot[3][:].rearrange("p (c n) -> p c n", c=2), ACT.Copy, scale=SCALE).then_inc(q_done, 1)
                    reached(act, q_mm, 2 * (t + 1) + 2)
                    nc.scalar.activation(q_t[1 - p][:, 2, :], slot[0][:, 0:2 * N], ACT.Copy, scale=SCALE).then_inc(q_done, 1)
                if now:
                    exps(t, 1, range(QUAD - 1))
                    for g in range(2):
                        if g == 1:
                            exps(t, 1, [QUAD - 1])
                        for c in range(PTC):
                            bank = slot[(3, 0, 1)[c]] if g == 0 else slot[c]
                            reached(act, pt_mm, PTC * (2 * t + g) + c + 1)
                            nc.scalar.activation(pt_hi[c][:], bank[:], ACT.Copy).then_inc(pt_hi_done, 1)
                    for g in range(2):
                        reached(act, ot_mm, 2 * t + g + 1)
                        nc.scalar.activation(ot_hi[g][:].rearrange("p c n -> p (c n)"), slot[3 * g][:, 0:D], ACT.Copy).then_inc(ot_hi_done, 1)

            attention_steps(act, step)

            def split_u_hi(b):
                reached(act, ut_mm, b + 1)
                nc.scalar.activation(ut_hi[:].rearrange("p c n -> p (c n)"), slot[2][:, 0:D], ACT.Copy).then_inc(ut_hi_done, 1)

            act.wait_ge(w1_loaded, 16 * E)
            act.wait_ge(wo_mm, B)
            for m in range(2 * E):
                if m >= E:
                    act.wait_ge(w2_loaded[m - E], 16)
                hi, lo = expert_weights(m)
                nc.scalar.activation(hi, lo.bitcast(F32), ACT.Copy).then_inc(split_hi, 1)
                if m == E - 1:
                    split_u_hi(0)
                if m == E + 1:
                    act.wait_ge(route_exp, 1)
                    nc.scalar.activation(g_tmp[:, 1, :], g_tmp[:, 0, :], ACT.Exp).then_inc(route_exp, 1)

            nc.scalar.preload_act_table(ACT.Gelu)
            act.wait_ge(routed, 1)
            at_ps = score[2:4]

            def choice(b, k):
                i = b * K + k
                cell = expert[0:1].rearrange("p b k -> p (b k)")
                cell = cell[:, i:i + 1] if isinstance(i, int) else cell[:, bass.ds(i, 1)]
                return act.value_load(cell, min_val=0, max_val=E - 1)

            def split_act_hi(b, k, m):
                i = b * K + k
                reached(act, at_mm, i + 1)
                col = (m * K + k) % 4
                for s in range(2):
                    nc.scalar.activation(at_hi[:, s * DC:(s + 1) * DC, :].rearrange("p c n -> p (c n)"), at_ps[s][:, 0:HALF],
                                         ACT.Copy, scale=gate_col[:, col, 1:2]).then_inc(at_hi_done, 1)

            def activate(b, k, e):
                i = b * K + k
                with act.If(e == SILU):
                    for s in range(2):
                        reached(act, hid_done, 2 * i + s + 1)
                        nc.scalar.activation(half_t[:, s], hid[k][:, s], ACT.Tanh, scale=0.5).then_inc(tanh_done, 1)
                    act.sem_inc(square_done, 1)
                    act.sem_inc(seed_half, 1)
                with act.Else():
                    with act.If(e == MISH):
                        for s in range(2):
                            reached(act, hid_done, 2 * i + s + 1)
                            nc.scalar.activation(half_t[:, s], hid[k][:, s], ACT.Tanh, scale=0.5).then_inc(tanh_done, 1)
                        act.wait_ge(tanh_done, 2 * i + 2)
                        nc.scalar.activation(half_t[:], half_t[:], ACT.Square, scale=-0.5, bias=half_col[:]).then_inc(square_done, 1)
                        act.wait_ge(square_done, i + 1)
                        nc.scalar.activation(inverse[:], half_t[:], ACT.Square, scale=SEED_G ** 0.5, bias=seed_in[:]).then_inc(seed_half, 1)
                    with act.Else():
                        for s in range(2):
                            reached(act, hid_done, 2 * i + s + 1)
                            nc.scalar.activation(hid[k][:, s], hid[k][:, s], ACT.Gelu).then_inc(a_ready[k], 1)
                        act.sem_inc(tanh_done, 2)
                        act.sem_inc(square_done, 1)
                        act.sem_inc(seed_half, 1)

            def invert(b, k, e):
                i = b * K + k
                with act.If(e == MISH):
                    act.wait_ge(seed_half, i + 1)
                    nc.scalar.activation(inverse[:], inverse[:], ACT.Square, bias=seed_out[:]).then_inc(seed_done, 1)
                    act.wait_ge(miss_done, i + 1)
                    nc.scalar.activation(miss2[:], half_t[:], ACT.Square, scale=-1.0, bias=one_col[:]).then_inc(miss2_done, 1)
                with act.Else():
                    act.sem_inc(seed_done, 1)
                    act.sem_inc(miss2_done, 1)

            def expert_step(b, m, lap):
                for k in range(K):
                    if k == 1 and graph(b, 1):
                        split_u_hi(b + 1)
                    if graph(b, 0):
                        e = choice(b, k)
                        activate(b, k, e)
                    if k == 0 and graph(b, -1):
                        split_act_hi(b - 1, 1, m - 1)
                    if k == 1 and graph(b, 0):
                        split_act_hi(b, 0, m)
                    if graph(b, 0):
                        invert(b, k, e)
                        if isinstance(b, int) and b == 0 and k == 0:
                            act.wait_ge(wide_loaded, 64)
                        scale_output_bias(b, k, m, e)

            def scale_output_bias(b, k, m, e):
                i = b * K + k
                col = (m * K + k) % 4
                reached(act, gate_copied, i + 1)
                reached(act, bias_half, i - 1)
                nc.scalar.activation(bias_part[k][:], b2_wide[:].rearrange("p e d -> p (e d)")[:, bass.ds(e * D, D)], ACT.Copy,
                                     scale=gate_col[:, col, 0:1]).then_inc(bias_scaled, 1)

            expert_steps(act, expert_step)

        @block.gpsimd
        def _(pool):
            nc.gpsimd.memset(ident[:], 0.0).then_inc(ident_ready, 1)
            nc.gpsimd.memset(neg_half[:], -0.5)
            nc.gpsimd.memset(half_col[:], 0.5)
            nc.gpsimd.memset(one_col[:], 1.0)
            nc.gpsimd.memset(seed_in[:], SEED_G ** 0.5 * SEED_B)
            nc.gpsimd.memset(seed_out[:], SEED_D)
            nc.gpsimd.memset(mean_w[:], 1.0 / N)
            for e in range(E):
                nc.gpsimd.memset(e_wide[:, e:e + 1], float(e))
                nc.gpsimd.memset(e_less[:, e:e + 1], float(e - E))
            for p in range(2):
                nc.gpsimd.memset(v_hi[p][:, :, :, HEAD:VW], 1.0)
                nc.gpsimd.memset(v_mid[p][:, :, :, HEAD:VW], 0.0)
                last = nc.gpsimd.memset(v_lo[p][:, :, :, HEAD:VW], 0.0)
            last.then_inc(const_ready, 1)
            pool.wait_ge(ident_ready, 1)
            nc.gpsimd.affine_select(out=ident[:], in_=ident[:], compare_op=ALU.not_equal, fill=1.0, base=0,
                                    pattern=[[-1, P]], channel_multiplier=1).then_inc(ident_ready, 1)
            pool.wait_ge(const_ready, 1)

            def inverse_root(out_, var, exponent, eps_done, count, done):
                nc.gpsimd.tensor_scalar(out_, var, EPS, None, ALU.add).then_inc(eps_done, 1)
                reached(pool, eps_done, count)
                nc.gpsimd.tensor_tensor(out_, out_, exponent, ALU.pow).then_inc(done, 1)

            def guard(t, g):
                n = 2 * t + g
                levels = N.bit_length() - 1
                reached(pool, max_ready, 4 * (n + 1))
                width = N // 2
                nc.gpsimd.tensor_tensor(fold[:], att[g][:, :, 0:width], att[g][:, :, width:N], ALU.add).then_inc(fold_done, 1)
                for level in range(1, levels):
                    reached(pool, fold_done, levels * n + level)
                    width //= 2
                    nc.gpsimd.tensor_tensor(fold[:, :, 0:width], fold[:, :, 0:width], fold[:, :, width:2 * width],
                                            ALU.add).then_inc(fold_done, 1)
                nc.gpsimd.tensor_scalar(zero_max[:], row_max[g][:], 0.0, None, ALU.is_equal).then_inc(zero_done, 1)
                reached_before(pool, fold_done, levels * (n + 1))
                nc.gpsimd.tensor_scalar(zero_sum[:], fold[:, :, 0], 0.0, None, ALU.is_equal).then_inc(zero_done, 1)
                reached(pool, zero_done, 4 * n + 2)
                nc.gpsimd.tensor_tensor(zero_sum[:], zero_sum[:], zero_max[:], ALU.mult).then_inc(zero_done, 1)
                reached_before(pool, zero_done, 4 * n + 3)
                nc.gpsimd.tensor_scalar(keep[g][:], zero_sum[:], -1.0, 1.0, ALU.mult, ALU.add).then_inc(zero_done, 1)
                reached_before(pool, zero_done, 4 * n + 4)
                nc.gpsimd.tensor_copy(keep[g][:, 0:1], keep[g][:, 0:1]).then_inc(keep_ready, 1)

            def step(t, p, lap):
                if has(t, 0):
                    for g in range(2):
                        reached(pool, v_hi_done, 2 * t + g + 1)
                        nc.gpsimd.tensor_tensor(heads(v_sum[g]), heads(v_sum[g]), v_hi[p][:, g, :, 0:HEAD], ALU.subtract).then_inc(v_rest_done, 1)
                    for g in range(2):
                        reached(pool, v_mid_done, 2 * t + g + 1)
                        nc.gpsimd.tensor_tensor(v_lo[p][:, g, :, 0:HEAD], heads(v_sum[g]), v_mid[p][:, g, :, 0:HEAD], ALU.subtract).then_inc(v_split, 1)
                if has(t, -1):
                    reached_before(pool, mv2_ready, 2 * t)
                    inverse_root(rs2[:, 1:2], mv2[:, 1, 1:2], neg_half[:, 0:1], rs2_eps, 2 * t, rs2_ready)
                if has(t, 2):
                    reached_before(pool, mv1_ready, t + 3)
                    inverse_root(rs1[:], mv1[:, :, 1], neg_half[:], rs1_eps, t + 3, rs1_ready)
                if has(t, 0):
                    guard(t, 0)
                    guard(t, 1)
                if isinstance(t, int) and t == -1:
                    pool.wait_ge(small_loaded, 16 * (3 + DC))
                if has(t, 1):
                    reached(pool, x_loaded[1 - p], 16 * (lap + 1 + p))
                    if has(t, -1):
                        reached(pool, u_ready, 2 * t)
                        reached(pool, x1_stored[1 - p], 16 * (lap + p))
                    for g in range(2):
                        last = nc.gpsimd.tensor_tensor(x1_sb[1 - p][:, g, :], x_in[1 - p][:, g, :], bo_wide[:], ALU.add)
                    last.then_inc(xbo_ready, 1)
                if has(t, 0):
                    reached_before(pool, mv2_ready, 2 * t + 1)
                    inverse_root(rs2[:, 0:1], mv2[:, 0, 1:2], neg_half[:, 0:1], rs2_eps, 2 * t + 1, rs2_ready)

            attention_steps(pool, step)

            def root_u(b):
                reached_before(pool, mv_u_ready, b + 1)
                inverse_root(rs_u[:], mv_u[:, 1:2], neg_half[:, 0:1], rs_u_eps, b + 1, rs_u_ready)

            root_u(0)
            for m in GPSIMD_SPLITS:
                hi, lo = expert_weights(m)
                pool.wait_ge(split_hi, m + 1)
                nc.gpsimd.tensor_tensor(lo, lo.bitcast(F32), hi.bitcast(F32), ALU.subtract).then_inc(gpsimd_lo, 1)
            pool.wait_ge(routed, 1)
            pool.wait_ge(wide_loaded, 64)

            def expert_step(b, m, lap):
                if graph(b, 1):
                    root_u(b + 1)
                if graph(b, -2):
                    d = (m - 2) % 4
                    reached_before(pool, mv_z_ready, b - 1)
                    inverse_root(rs_z[:], mv_z[:, 1:2], neg_half[:, 0:1], rs_z_eps, b - 1, rs_z_ready)
                    reached(pool, zn_done, b - 1)
                    nc.gpsimd.tensor_tensor(z_sb[d][:], z_sb[d][:], lng_wide[:], ALU.mult).then_inc(zg_done, 1)
                    reached(pool, zg_done, b - 1)
                    nc.gpsimd.tensor_tensor(z_sb[d][:], z_sb[d][:], x1_in[d][:], ALU.add).then_inc(zx_done, 1)
                    reached(pool, zx_done, b - 1)
                    nc.gpsimd.tensor_tensor(z_sb[d][:], z_sb[d][:], lnb_wide[:], ALU.add).then_inc(out_ready, 1)

                if graph(b, 0):
                    for k in range(K):
                        i = b * K + k
                        reached(pool, bias_half, i)
                        reached(pool, bias_scaled, i + 1)
                        reached(pool, ut_mm, b + 1)
                        nc.gpsimd.tensor_tensor(z_sb[m][:], z_sb[m][:], bias_part[k][:], ALU.add).then_inc(bias_half, 1)

            expert_steps(pool, expert_step)

        @block.vector
        def _(dve):
            def add_bias_and_max(t, p, g, lap, before_last=None):
                n = 2 * t + g
                reached(dve, adj_loaded[p], 16 * (lap + 1))
                for r in range(QUAD):
                    if r == QUAD - 1 and before_last:
                        before_last()
                    reached_before(dve, s_mm, 4 * n + r + 1)
                    for c in range(DC):
                        hh = r * DC + c
                        last = nc.vector.tensor_tensor_reduce(out=att[g][:, hh, :], in0=score[r][:, c * N:(c + 1) * N], in1=adj_in[p][:, g, :],
                                                              scale=1.0, scalar=LOWEST, op0=ALU.add, op1=ALU.max,
                                                              accum_out=row_max[g][:, hh:hh + 1])
                    last.then_inc(max_ready, 1)
                    reached(dve, max_ready, 4 * n + r + 1)
                    nc.vector.tensor_scalar(neg_max[g][:, r * DC:(r + 1) * DC], row_max[g][:, r * DC:(r + 1) * DC],
                                            -1.0, None, ALU.mult).then_inc(neg_ready, 1)

            def residual(t, g, p, bank):
                n = 2 * t + g
                reached(dve, wo_mm, n + 1)
                reached(dve, xbo_ready, t + 1)
                nc.vector.tensor_tensor(x1_sb[p][:, g, :], bank[:, 0:D], x1_sb[p][:, g, :], ALU.add).then_inc(x1_done, 1)
                reached(dve, x1_done, n + 1)
                nc.vector.bn_stats(st2[:, g, :], x1_sb[p][:, g, :]).then_inc(st2_done, 1)
                reached_before(dve, st2_done, n + 1)
                nc.vector.bn_aggr(mv2[:, g, :], st2[:, g, :]).then_inc(mv2_ready, 1)

            def normalise_x1(t, g, p):
                reached(dve, rs2_ready, 2 * t + g + 1)
                nc.vector.tensor_scalar(u_att[:, g, :], x1_sb[p][:, g, :], mv2[:, g, 0:1], rs2[:, g:g + 1],
                                        ALU.subtract, ALU.mult).then_inc(u_ready, 1)

            def split_prob_lo(t, g, c, bank):
                reached(dve, pt_hi_done, PTC * (2 * t + g) + c + 1)
                nc.vector.tensor_tensor(pt_lo[c][:], bank[:], pt_hi[c][:], ALU.subtract).then_inc(pt_done, 1)

            def take_v(t, g, bank):
                reached(dve, v_mm, 2 * t + g + 1)
                reached(dve, v_split, 2 * t + g - 1)
                nc.vector.tensor_tensor(v_sum[g][:], bank[:, 0:D], bv_wide[:], ALU.add).then_inc(v_done, 1)

            def divide(t, g, bank):
                n = 2 * t + g
                reached(dve, o_mm, n + 1)
                o_ps = bank[:, 0:HEADS * VW].rearrange("p (h d) -> p h d", d=VW)
                nc.vector.reciprocal(inv_sum[g][:], o_ps[:, :, HEAD]).then_inc(inv_done, 1)
                reached(dve, inv_done, n + 1)
                reached(dve, keep_ready, n + 1)
                nc.vector.tensor_tensor(inv_kept[g][:], inv_sum[g][:], keep[g][:], ALU.mult).then_inc(kept_done, 1)
                reached(dve, kept_done, n + 1)
                nc.vector.tensor_tensor(o_sb[g][:].rearrange("p (c r d) -> p r c d", c=DC, r=QUAD),
                                        o_ps[:, :, 0:HEAD].rearrange("p (r c) d -> p r c d", r=QUAD),
                                        inv_kept[g][:].rearrange("p (r c o) -> p r c o", r=QUAD, o=1).to_broadcast([P, QUAD, DC, HEAD]),
                                        ALU.mult).then_inc(o_done, 1)

            def take_means(t, bank):
                reached(dve, pooled_mm, t + 1)
                where = slice(2 * t, 2 * t + 2) if isinstance(t, int) else bass.ds(t * 2, 2)
                first = HEADS * VW
                nc.vector.tensor_copy(pooled[:, where, :], bank[:, first:first + 2 * DC].rearrange("p (g c) -> p g c", g=2)).then_inc(pooled_done, 1)

            def split_o_lo(t, g, bank):
                reached(dve, ot_hi_done, 2 * t + g + 1)
                nc.vector.tensor_tensor(ot_lo[g][:].rearrange("p c n -> p (c n)"), bank[:, 0:D],
                                        ot_hi[g][:].rearrange("p c n -> p (c n)").bitcast(F32), ALU.subtract).then_inc(ot_lo_done, 1)

            def step(t, p, lap):
                now, nxt, prev, far = has(t, 0), has(t, 1), has(t, -1), has(t, 2)
                if isinstance(t, int) and t == -1:
                    for n in range(4 * DC):
                        dve.wait_ge(wt_hi_done, n + 1)
                        nc.vector.tensor_tensor(wt_lo[n // DC][:, n % DC, :], slot[n % 4][:, 0:D],
                                                wt_hi[n // DC][:, n % DC, :].bitcast(F32), ALU.subtract).then_inc(wt_lo_done, 1)
                    dve.wait_ge(small_loaded, 16 * (3 + DC))
                if isinstance(t, int) and t == 1:
                    nc.vector.tensor_copy(rw_wide[:].rearrange("p c e n -> p (c e) n"),
                                          rw_t[:].rearrange("p c (e o) -> p (c e) o", o=1).to_broadcast([P, DC * E, P])).then_inc(const_ready, 1)
                if nxt:
                    reached(dve, xt_hi_done, 2 * (t + 1) + 1)
                    nc.vector.tensor_tensor(xt_lo[:, 0:2, :], slot[0][:].rearrange("p (c n) -> p c n", c=2),
                                            xt_hi[:, 0:2, :].bitcast(F32), ALU.subtract).then_inc(xt_lo_done, 1)
                    reached(dve, xt_hi_done, 2 * (t + 1) + 2)
                    nc.vector.tensor_tensor(xt_lo[:, 2, :], slot[1][:, 0:2 * N], xt_hi[:, 2, :].bitcast(F32),
                                            ALU.subtract).then_inc(xt_lo_done, 1)
                if now:
                    add_bias_and_max(t, p, 0, lap)
                if prev:
                    residual(t - 1, 1, 1 - p, slot[2])
                if far:
                    reached(dve, x_loaded[p], 16 * (lap + 2))
                    for g in range(2):
                        last = nc.vector.bn_stats(st1[:, g, :], x_in[p][:, g, :])
                    last.then_inc(st1_done, 1)
                    reached_before(dve, st1_done, t + 3)
                    for g in range(2):
                        last = nc.vector.bn_aggr(mv1[:, g, :], st1[:, g, :])
                    last.then_inc(mv1_ready, 1)

                def take_k():
                    reached(dve, k_mm, 2 * (t + 1) + 1)
                    nc.vector.tensor_copy(k_t[1 - p][:, 0:2, :], slot[1][:].rearrange("p (c n) -> p c n", c=2)).then_inc(k_done, 1)

                if now:
                    add_bias_and_max(t, p, 1, lap, before_last=take_k if nxt else None)
                elif nxt:
                    take_k()
                if nxt:
                    reached(dve, k_mm, 2 * (t + 1) + 2)
                    nc.vector.tensor_copy(k_t[1 - p][:, 2, :], slot[2][:, 0:2 * N]).then_inc(k_done, 1)
                if now:
                    for c in range(PTC):
                        split_prob_lo(t, 0, c, slot[(3, 0, 1)[c]])
                if nxt:
                    take_v(t + 1, 0, slot[2])
                if prev:
                    normalise_x1(t - 1, 1, 1 - p)
                if now:
                    divide(t, 0, slot[3])
                if now:
                    for c in range(PTC):
                        split_prob_lo(t, 1, c, slot[c])
                if nxt:
                    take_v(t + 1, 1, slot[3])
                if now:
                    split_o_lo(t, 0, slot[0])
                if far:
                    reached(dve, rs1_ready, t + 3)
                    for g in range(2):
                        last = nc.vector.tensor_scalar(xn[:, g, :], x_in[p][:, g, :], mv1[:, g, 0:1], rs1[:, g:g + 1],
                                                       ALU.subtract, ALU.mult)
                    last.then_inc(xn_ready, 1)
                if now:
                    reached(dve, o_mm, 2 * t + 2)
                if prev:
                    take_means(t - 1, slot[1])
                if now:
                    divide(t, 1, slot[1])
                    residual(t, 0, p, slot[2])
                    split_o_lo(t, 1, slot[3])
                    normalise_x1(t, 0, p)

            attention_steps(dve, step)

            hid_ps, at_ps, y_ps, ut_ps = score[0:2], score[2:4], slot[0:2], slot[2]

            def choice(b, k):
                i = b * K + k
                cell = expert[0:1].rearrange("p b k -> p (b k)")
                cell = cell[:, i:i + 1] if isinstance(i, int) else cell[:, bass.ds(i, 1)]
                return dve.value_load(cell, min_val=0, max_val=E - 1)

            def stats_u(b, m, lap):
                reached(dve, x1_loaded[m], 16 * (lap + 1))
                nc.vector.bn_stats(st_u[:], x1_in[m][:]).then_inc(st_u_done, 1)
                reached_before(dve, st_u_done, b + 1)
                nc.vector.bn_aggr(mv_u[:], st_u[:]).then_inc(mv_u_ready, 1)

            def normalise_u(b, m, lap):
                reached(dve, rs_u_ready, b + 1)
                reached(dve, out_stored[m], 16 * lap)
                nc.vector.tensor_scalar(z_sb[m][:], x1_in[m][:], mv_u[:, 0:1], rs_u[:], ALU.subtract, ALU.mult).then_inc(un_ready, 1)

            def split_u_lo(b):
                reached(dve, ut_hi_done, b + 1)
                nc.vector.tensor_tensor(ut_lo[:].rearrange("p c n -> p (c n)"), ut_ps[:, 0:D],
                                        ut_hi[:].rearrange("p c n -> p (c n)").bitcast(F32), ALU.subtract).then_inc(ut_lo_done, 1)

            def split_act_lo(b, k, m):
                i = b * K + k
                col = (m * K + k) % 4
                for s in range(2):
                    reached(dve, at_hi_done, 2 * i + s + 1)
                    nc.vector.scalar_tensor_tensor(out=at_lo[:, s * DC:(s + 1) * DC, :].rearrange("p c n -> p (c n)"), in0=at_ps[s][:, 0:HALF],
                                                   scalar=gate_col[:, col, 1:2],
                                                   in1=at_hi[:, s * DC:(s + 1) * DC, :].rearrange("p c n -> p (c n)").bitcast(F32),
                                                   op0=ALU.mult, op1=ALU.subtract).then_inc(at_lo_done, 1)

            def take_hidden(b, k, m, e):
                i = b * K + k
                col = (m * K + k) % 4
                g = gate[:].rearrange("p b k f -> p (b k f)")
                g = g[:, 2 * i:2 * i + 2] if isinstance(i, int) else g[:, bass.ds(i * 2, 2)]
                nc.vector.tensor_copy(gate_col[:, col, :], g).then_inc(gate_copied, 1)
                reached(dve, h_mm, i + 1)
                for s in range(2):
                    nc.vector.tensor_tensor(hid[k][:, s], hid_ps[s][:, 0:HALF],
                                            b1_wide[:].rearrange("p e s f -> p (e s f)")[:, bass.ds(e * F + s * HALF, HALF)],
                                            ALU.add).then_inc(hid_done, 1)

            def activate_first(b, k, e):
                i = b * K + k
                with dve.If(e == SILU):
                    for s in range(2):
                        dve.wait_ge(tanh_done, 2 * i + s + 1)
                        nc.vector.scalar_tensor_tensor(out=hid[k][:, s], in0=half_t[:, s], scalar=1.0, in1=hid[k][:, s],
                                                       op0=ALU.add, op1=ALU.mult).then_inc(a_ready[k], 1)
                with dve.Else():
                    dve.nop()

            def activate_second(b, k, e):
                i = b * K + k
                with dve.If(e == MISH):
                    dve.wait_ge(seed_done, i + 1)
                    nc.vector.scalar_tensor_tensor(out=half_t[:], in0=half_t[:], scalar=1.0, in1=inverse[:],
                                                   op0=ALU.add, op1=ALU.mult).then_inc(miss_done, 1)
                    dve.wait_ge(miss_done, i + 1)
                    nc.vector.scalar_tensor_tensor(out=inverse[:], in0=half_t[:], scalar=2.0, in1=inverse[:],
                                                   op0=ALU.subtract, op1=ALU.mult).then_inc(newton_done, 1)
                    dve.wait_ge(newton_done, i + 1)
                    dve.wait_ge(miss2_done, i + 1)
                    nc.vector.scalar_tensor_tensor(out=inverse[:], in0=miss2[:], scalar=1.0, in1=inverse[:],
                                                   op0=ALU.add, op1=ALU.mult).then_inc(inverse_done, 1)
                    dve.wait_ge(inverse_done, i + 1)
                    for s in range(2):
                        nc.vector.scalar_tensor_tensor(out=hid[k][:, s], in0=inverse[:, s], scalar=0.5, in1=hid[k][:, s],
                                                       op0=ALU.add, op1=ALU.mult).then_inc(a_ready[k], 1)
                with dve.Else():
                    dve.sem_inc(miss_done, 1)
                    dve.sem_inc(newton_done, 1)
                    dve.sem_inc(inverse_done, 1)

            def add_experts(b, m):
                reached(dve, y_mm, K * (b + 1))
                reached(dve, bias_half, K * (b + 1))
                nc.vector.tensor_tensor(z_sb[m][:], y_ps[m % 2][:, 0:D], z_sb[m][:], ALU.add).then_inc(z_added, 1)
                reached(dve, z_added, b + 1)
                nc.vector.bn_stats(st_z[:], z_sb[m][:]).then_inc(st_z_done, 1)
                reached_before(dve, st_z_done, b + 1)
                nc.vector.bn_aggr(mv_z[:], st_z[:]).then_inc(mv_z_ready, 1)

            def normalise_z(b, m):
                reached(dve, rs_z_ready, b + 1)
                nc.vector.tensor_scalar(z_sb[m][:], z_sb[m][:], mv_z[:, 0:1], rs_z[:], ALU.subtract, ALU.mult).then_inc(zn_done, 1)

            def split_weights_lo(m):
                hi, lo = expert_weights(m)
                dve.wait_ge(split_hi, m + 1)
                nc.vector.tensor_tensor(lo, lo.bitcast(F32), hi.bitcast(F32), ALU.subtract).then_inc(vector_lo, 1)

            steps = [0]

            def chained(instruction):
                steps[0] += 1
                instruction.then_inc(route_step, 1)
                dve.wait_ge(route_step, steps[0])

            def over_experts(v):
                return v.rearrange("p (b o) -> p b o", o=1).to_broadcast([P, B, E])

            def over_graphs(v):
                return v.rearrange("p (o e) -> p o e", o=1).to_broadcast([P, B, E])

            stats_u(0, 0, 0)
            for m in VECTOR_SPLITS:
                if m < E:
                    split_weights_lo(m)
            dve.wait_ge(logit_mm, 1)
            chained(nc.vector.tensor_tensor(logit[:], slot[0][:, 0:E * B].rearrange("p (e b) -> p b e", e=E), over_graphs(rb_wide[:]), ALU.add))
            normalise_u(0, 0, 0)
            for k in range(K):
                chained(nc.vector.tensor_reduce(top[:, k, :], logit[:], AX.X, ALU.max))
                chained(nc.vector.tensor_tensor(hit[:], logit[:], over_experts(top[:, k, :]), ALU.is_equal))
                chained(nc.vector.tensor_tensor(hit[:], hit[:], over_graphs(e_less[:]), ALU.mult))
                chained(nc.vector.tensor_reduce(top_e[:, k, :], hit[:], AX.X, ALU.min))
                chained(nc.vector.tensor_scalar(top_e[:, k, :], top_e[:, k, :], float(E), None, ALU.add))
                chained(nc.vector.tensor_copy(expert[:, :, k], top_e[:, k, :]))
                if k == 0:
                    split_u_lo(0)
                    chained(nc.vector.tensor_tensor(hit[:], over_graphs(e_wide[:]), over_experts(top_e[:, k, :]), ALU.is_equal))
                    chained(nc.vector.scalar_tensor_tensor(out=logit[:], in0=hit[:], scalar=LOWEST, in1=logit[:], op0=ALU.mult, op1=ALU.add))
            nc.vector.tensor_tensor(g_tmp[:, 0, :], top[:, 1, :], top[:, 0, :], ALU.subtract).then_inc(route_exp, 1)
            numbers = top_e[:]
            chained(nc.vector.tensor_scalar(factor[:, 0], numbers, float(SILU), -0.5, ALU.is_equal, ALU.mult))
            chained(nc.vector.tensor_scalar(factor[:, 1], numbers, float(MISH), -3.0, ALU.is_equal, ALU.mult))
            chained(nc.vector.scalar_tensor_tensor(out=factor[:, 0], in0=factor[:, 0], scalar=1.0, in1=factor[:, 1], op0=ALU.add, op1=ALU.add))
            dve.wait_ge(route_exp, 2)
            chained(nc.vector.tensor_scalar(g_tmp[:, 2, :], g_tmp[:, 1, :], 1.0, None, ALU.add))
            chained(nc.vector.reciprocal(g_tmp[:, 0, :], g_tmp[:, 2, :]))
            chained(nc.vector.tensor_copy(gate[:, :, 0, 0], g_tmp[:, 0, :]))
            chained(nc.vector.tensor_tensor(gate[:, :, 1, 0], g_tmp[:, 0, :], g_tmp[:, 1, :], ALU.mult))
            nc.vector.tensor_tensor(gate[:, :, :, 1], gate[:, :, :, 0], factor[:, 0].rearrange("p k b -> p b k"), ALU.mult).then_inc(routed, 1)
            for m in VECTOR_SPLITS:
                if m >= E:
                    split_weights_lo(m)
            dve.wait_ge(routed, 1)

            def expert_step(b, m, lap):
                for k in range(K):
                    if graph(b, 0):
                        if isinstance(b, int) and b == 0 and k == 0:
                            dve.wait_ge(wide_loaded, 64)
                        e = choice(b, k)
                        take_hidden(b, k, m, e)
                    if k == 0 and graph(b, 1):
                        stats_u(b + 1, (m + 1) % 4, lap + (m + 1) // 4)
                    if k == 1 and graph(b, 1):
                        split_u_lo(b + 1)
                    if k == 0 and graph(b, -2):
                        add_experts(b - 2, (m - 2) % 4)
                    if k == 0 and graph(b, 1):
                        normalise_u(b + 1, (m + 1) % 4, lap + (m + 1) // 4)
                    if graph(b, 0):
                        activate_first(b, k, e)
                    if k == 0 and graph(b, -1):
                        split_act_lo(b - 1, 1, m - 1)
                    if k == 1 and graph(b, 0):
                        split_act_lo(b, 0, m)
                    if graph(b, 0):
                        activate_second(b, k, e)
                    if k == 0 and graph(b, -2):
                        normalise_z(b - 2, (m - 2) % 4)

            expert_steps(dve, expert_step)


_INS = ["x", "adj", "L0_gnn_Wq", "L0_gnn_Wk", "L0_gnn_Wv", "L0_gnn_bv", "L0_gnn_Wo", "L0_gnn_bo", "L0_ffn_router_w",
        "L0_ffn_router_b", "L0_ffn_w1", "L0_ffn_b1", "L0_ffn_w2", "L0_ffn_b2", "L0_ffn_ln_g", "L0_ffn_ln_b"]


def kernel(**inputs):
    import numpy as np
    import concourse.bacc as bacc
    from concourse.bass_utils import run_bass_kernel_spmd

    nc = bacc.Bacc("TRN2", target_bir_lowering=False, num_devices=1)
    arrays, args = {}, []
    for name in _INS:
        a = np.ascontiguousarray(inputs[name])
        arrays[f"in_{name}"] = a
        args.append(nc.dram_tensor(f"in_{name}", a.shape, mybir.dt.from_np(a.dtype), kind="ExternalInput").ap())
    out = nc.dram_tensor("out_dram", inputs["x"].shape, F32, kind="ExternalOutput").ap()
    gnn_moe_kernel(nc, *args, out)
    r = run_bass_kernel_spmd(nc, [arrays], core_ids=[0])
    return r.results[0]["out_dram"]
```
